# Optimizing a Trainium2 kernel written in Bass

```python
import numpy as np
import jax
import jax.numpy as jnp

def _softmax(x, axis=-1):
    return jax.nn.softmax(x, axis=axis)

def _gelu(x):
    return jax.nn.gelu(x, approximate=True)

def _silu(x):
    return jax.nn.silu(x)

def _sigmoid(x):
    return jax.nn.sigmoid(x)

def _layernorm(x, axis=-1, eps=1e-05):
    m = jnp.mean(x, axis=axis, keepdims=True)
    v = jnp.var(x, axis=axis, keepdims=True)
    return (x - m) / jnp.sqrt(v + eps)

def _scatter_add(tgt, idx, src, axis=0):
    return tgt.at[idx].add(src)

def _segment_sum(src, seg, n):
    return jax.ops.segment_sum(src, seg, n)
kernel_name = 'mk_hybrid_d1_jaxref_r4_74d2f4'

def setup_inputs(seed: int=0):
    np.random.seed(seed)
    _w = jnp.asarray

    def _L0_attn_a_setup():
        import jax, jax.numpy as jnp
        import numpy as np
        import math
        INPUT_WIDTH = 256
        KEY_WIDTH = 64
        VALUE_WIDTH = 64
        NUM_HEADS = 16
        key = jax.random.key(seed)
        k_x, k_q, k_k, k_v, k_p = jax.random.split(key, 5)
        n, s = (2, 512)
        scale = 1.0 / math.sqrt(INPUT_WIDTH)
        X = jax.random.normal(k_x, (n, s, INPUT_WIDTH), dtype=jnp.float32)
        Wq = jax.random.uniform(k_q, (INPUT_WIDTH, NUM_HEADS * KEY_WIDTH), jnp.float32, -scale, scale)
        Wk = jax.random.uniform(k_k, (INPUT_WIDTH, NUM_HEADS * KEY_WIDTH), jnp.float32, -scale, scale)
        Wv = jax.random.uniform(k_v, (INPUT_WIDTH, NUM_HEADS * VALUE_WIDTH), jnp.float32, -scale, scale)
        p_scale = 1.0 / math.sqrt(NUM_HEADS * VALUE_WIDTH)
        Wpost = jax.random.uniform(k_p, (NUM_HEADS * VALUE_WIDTH, INPUT_WIDTH), jnp.float32, -p_scale, p_scale)
        return {'X': X, 'Wq': Wq, 'Wk': Wk, 'Wv': Wv, 'Wpost': Wpost}
    _L0_attn_a_in = _L0_attn_a_setup()

    def _L0_attn_b_setup():
        import jax, jax.numpy as jnp
        import numpy as np
        NUM_HEADS = 16
        EMBED_DIM = 256
        HEAD_DIM = EMBED_DIM // NUM_HEADS
        ROPE_BASE = 10000.0

        def _split_heads(x):
            B, T, _ = x.shape
            return x.reshape(B, T, NUM_HEADS, HEAD_DIM).transpose(0, 2, 1, 3)

        def _rope(q, k):
            T = q.shape[-2]
            half = HEAD_DIM // 2
            dtype = q.dtype
            pos = jnp.arange(T, dtype=dtype)[:, None]
            idx = jnp.arange(half, dtype=dtype)[None, :]
            inv_freq = 1.0 / ROPE_BASE ** (idx / jnp.asarray(half, dtype))
            angles = pos * inv_freq
            sin = jnp.sin(angles)[None, None]
            cos = jnp.cos(angles)[None, None]

            def rot(x):
                x1, x2 = jnp.split(x, 2, axis=-1)
                return jnp.concatenate([x1 * cos - x2 * sin, x1 * sin + x2 * cos], axis=-1)
            return (rot(q), rot(k))
        key = jax.random.key(seed)
        ks = jax.random.split(key, 5)
        B, T, D = (2, 512, EMBED_DIM)
        s = 1.0 / np.sqrt(D)
        return {'x': jax.random.normal(ks[0], (B, T, D), jnp.float32), 'wq_w': jax.random.normal(ks[1], (D, D), jnp.float32) * s, 'wq_b': jnp.zeros((D,), jnp.float32), 'wk_w': jax.random.normal(ks[2], (D, D), jnp.float32) * s, 'wk_b': jnp.zeros((D,), jnp.float32), 'wv_w': jax.random.normal(ks[3], (D, D), jnp.float32) * s, 'wv_b': jnp.zeros((D,), jnp.float32), 'wo_w': jax.random.normal(ks[4], (D, D), jnp.float32) * s, 'wo_b': jnp.zeros((D,), jnp.float32)}
    _L0_attn_b_in = _L0_attn_b_setup()

    def _L0_ffn_setup():
        import jax, jax.numpy as jnp
        import numpy as np
        EPS = 1e-05

        def _quantize(W):
            gamma = jnp.mean(jnp.abs(W))
            return jnp.clip(jnp.round(W / (gamma + EPS)), -1.0, 1.0)
        key = jax.random.key(seed)
        k_x, k_w1, k_b1, k_w2, k_b2 = jax.random.split(key, 5)
        n_embd = 256
        d_ff = 4 * n_embd
        B, S = (4, 1024)
        bound1 = 1.0 / np.sqrt(n_embd)
        bound2 = 1.0 / np.sqrt(d_ff)
        x = jax.random.normal(k_x, (B, S, n_embd), dtype=jnp.float32)
        W1 = jax.random.uniform(k_w1, (d_ff, n_embd), jnp.float32, -bound1, bound1)
        b1 = jax.random.uniform(k_b1, (d_ff,), jnp.float32, -bound1, bound1)
        W2 = jax.random.uniform(k_w2, (n_embd, d_ff), jnp.float32, -bound2, bound2)
        b2 = jax.random.uniform(k_b2, (n_embd,), jnp.float32, -bound2, bound2)
        return {'x': x, 'W1': W1, 'b1': b1, 'W2': W2, 'b2': b2}
    _L0_ffn_in = _L0_ffn_setup()
    _d = {'L0_attn_a_X': _L0_attn_a_in['X'], 'L0_attn_a_Wq': _L0_attn_a_in['Wq'], 'L0_attn_a_Wk': _L0_attn_a_in['Wk'], 'L0_attn_a_Wv': _L0_attn_a_in['Wv'], 'L0_attn_a_Wpost': _L0_attn_a_in['Wpost'], 'L0_attn_b_wq_w': _L0_attn_b_in['wq_w'], 'L0_attn_b_wq_b': _L0_attn_b_in['wq_b'], 'L0_attn_b_wk_w': _L0_attn_b_in['wk_w'], 'L0_attn_b_wk_b': _L0_attn_b_in['wk_b'], 'L0_attn_b_wv_w': _L0_attn_b_in['wv_w'], 'L0_attn_b_wv_b': _L0_attn_b_in['wv_b'], 'L0_attn_b_wo_w': _L0_attn_b_in['wo_w'], 'L0_attn_b_wo_b': _L0_attn_b_in['wo_b'], 'L0_ffn_W1': _L0_ffn_in['W1'], 'L0_ffn_b1': _L0_ffn_in['b1'], 'L0_ffn_W2': _L0_ffn_in['W2'], 'L0_ffn_b2': _L0_ffn_in['b2']}
    _x0 = _d['L0_attn_a_X']
    _d['L0_attn_a_X'] = jax.random.normal(jax.random.fold_in(jax.random.key(seed), 1), (16, 512, 256), dtype=_x0.dtype)
    del _x0
    return _d

def reference(L0_attn_a_X, L0_attn_a_Wq, L0_attn_a_Wk, L0_attn_a_Wv, L0_attn_a_Wpost, L0_attn_b_wq_w, L0_attn_b_wq_b, L0_attn_b_wk_w, L0_attn_b_wk_b, L0_attn_b_wv_w, L0_attn_b_wv_b, L0_attn_b_wo_w, L0_attn_b_wo_b, L0_ffn_W1, L0_ffn_b1, L0_ffn_W2, L0_ffn_b2):

    def _L0_attn_a_ref(X, Wq, Wk, Wv, Wpost):
        import jax, jax.numpy as jnp
        import numpy as np
        import math
        INPUT_WIDTH = 256
        KEY_WIDTH = 64
        VALUE_WIDTH = 64
        NUM_HEADS = 16
        n, s, _ = X.shape
        Q = (X @ Wq).reshape(n, s, NUM_HEADS, KEY_WIDTH)
        K = (X @ Wk).reshape(n, s, NUM_HEADS, KEY_WIDTH)
        V = (X @ Wv).reshape(n, s, NUM_HEADS, VALUE_WIDTH)
        inv_sqrt_d = 1.0 / math.sqrt(KEY_WIDTH)
        raw_attn = jnp.einsum('bshe,bthe->bsth', Q, K * inv_sqrt_d)
        attn = jax.nn.softmax(raw_attn, axis=2)
        A = jnp.einsum('bsth,bthe->bshe', attn, V).reshape(n, s, NUM_HEADS * VALUE_WIDTH)
        A = jax.nn.gelu(A, approximate=False)
        P = A @ Wpost
        return X + P

    def _L0_attn_b_ref(x, wq_w, wq_b, wk_w, wk_b, wv_w, wv_b, wo_w, wo_b):
        import jax, jax.numpy as jnp
        import numpy as np
        NUM_HEADS = 16
        EMBED_DIM = 256
        HEAD_DIM = EMBED_DIM // NUM_HEADS
        ROPE_BASE = 10000.0

        def _split_heads(x):
            B, T, _ = x.shape
            return x.reshape(B, T, NUM_HEADS, HEAD_DIM).transpose(0, 2, 1, 3)

        def _rope(q, k):
            T = q.shape[-2]
            half = HEAD_DIM // 2
            dtype = q.dtype
            pos = jnp.arange(T, dtype=dtype)[:, None]
            idx = jnp.arange(half, dtype=dtype)[None, :]
            inv_freq = 1.0 / ROPE_BASE ** (idx / jnp.asarray(half, dtype))
            angles = pos * inv_freq
            sin = jnp.sin(angles)[None, None]
            cos = jnp.cos(angles)[None, None]

            def rot(x):
                x1, x2 = jnp.split(x, 2, axis=-1)
                return jnp.concatenate([x1 * cos - x2 * sin, x1 * sin + x2 * cos], axis=-1)
            return (rot(q), rot(k))
        B, T, D = x.shape
        q = _split_heads(x @ wq_w + wq_b)
        k = _split_heads(x @ wk_w + wk_b)
        v = _split_heads(x @ wv_w + wv_b)
        q, k = _rope(q, k)
        scale = HEAD_DIM ** (-0.5)
        logits = jnp.einsum('bhqd,bhkd->bhqk', q, k) * scale
        attn = jax.nn.softmax(logits, axis=-1)
        y = jnp.einsum('bhqk,bhkd->bhqd', attn, v)
        y = y.transpose(0, 2, 1, 3).reshape(B, T, D)
        return y @ wo_w + wo_b

    def _L0_ffn_ref(x, W1, b1, W2, b2):
        import jax, jax.numpy as jnp
        import numpy as np
        EPS = 1e-05

        def _quantize(W):
            gamma = jnp.mean(jnp.abs(W))
            return jnp.clip(jnp.round(W / (gamma + EPS)), -1.0, 1.0)
        Wq1 = _quantize(W1)
        Wq2 = _quantize(W2)
        h = jax.nn.relu(jnp.einsum('bsd,fd->bsf', x, Wq1) + b1)
        out = jnp.einsum('bsf,df->bsd', h, Wq2) + b2
        return out
    x = L0_attn_a_X
    x = x + _L0_attn_a_ref(_layernorm(x, axis=-1), L0_attn_a_Wq, L0_attn_a_Wk, L0_attn_a_Wv, L0_attn_a_Wpost)
    x = x + _L0_ffn_ref(_layernorm(x, axis=-1), L0_ffn_W1, L0_ffn_b1, L0_ffn_W2, L0_ffn_b2)
    x = x + _L0_attn_b_ref(_layernorm(x, axis=-1), L0_attn_b_wq_w, L0_attn_b_wq_b, L0_attn_b_wk_w, L0_attn_b_wk_b, L0_attn_b_wv_w, L0_attn_b_wv_b, L0_attn_b_wo_w, L0_attn_b_wo_b)
    x = x + _L0_ffn_ref(_layernorm(x, axis=-1), L0_ffn_W1, L0_ffn_b1, L0_ffn_W2, L0_ffn_b2)
    return x

_drawn_inputs = setup_inputs


def setup_inputs(seed=0):
    import zlib

    import numpy as np

    out = dict(_drawn_inputs(seed))
    spreads = {'L0_attn_b_wq_b': (0.0, 0.8),
     'L0_attn_b_wk_b': (0.0, 0.8),
     'L0_attn_b_wv_b': (0.0, 2.0),
     'L0_attn_b_wo_b': (0.0, 2.0)}
    factors = {'L0_attn_a_Wq': 8.0,
     'L0_attn_a_Wk': 8.0,
     'L0_attn_a_Wv': 8.0,
     'L0_attn_a_Wpost': 8.0,
     'L0_attn_b_wq_w': 8.0,
     'L0_attn_b_wk_w': 8.0,
     'L0_attn_b_wv_w': 8.0,
     'L0_attn_b_wo_w': 8.0,
     'L0_ffn_b1': 8.0,
     'L0_ffn_b2': 200.0}
    for name, (base, spread) in spreads.items():
        noise = np.random.default_rng([zlib.crc32(name.encode()), seed]).standard_normal(out[name].shape)
        drawn = base * np.exp(spread * noise) if base else spread * noise
        out[name] = jnp.asarray(drawn.astype(out[name].dtype))
    for name, factor in factors.items():
        out[name] = (out[name] * factor).astype(out[name].dtype)
    return out
```

```python
import concourse.bass as bass
from concourse import mybir
from contextlib import ExitStack



def hybrid_block_kernel(nc, X, WQ, WK, WV, WPOST, WB, BQK, BV, WO, BO, W1T, B1, W2T, B2, COS, SIN, OUT):
    F32, F32R = mybir.dt.float32, mybir.dt.float32r
    ALU = mybir.AluOpType
    ACT = mybir.ActivationFunctionType
    AX = mybir.AxisListType

    P = 128
    BATCH, S, D = X.shape
    TB = S // P
    KT = D // P
    DA = WQ.shape[1]
    H = 16
    HA = DA // H
    HB = D // H
    PAIRS = H // 2
    FF = W1T.shape[1]
    FT = FF // P
    QUADS = H // 4
    EPS = 1e-5
    SCALE_A = float(HA) ** -0.5
    SCALE_B = float(HB) ** -0.5
    UNITS = 2 * H
    HS = S // 2

    ctx = ExitStack()
    with ctx:
        KB = 1024

        def sb(name, shape, dt=F32):
            return ctx.enter_context(nc.sbuf_tensor(name, shape, dt))

        wa_hi = sb("wa_hi", [P, KT, 3 * DA], F32R)
        wa_lo = sb("wa_lo", [P, KT, 3 * DA], F32R)
        wpost = sb("wpost", [P, DA // P, D])
        w1 = sb("w1", [P, KT, FF], F32R)
        w2 = sb("w2", [P, FT, D], F32R)
        wb_hi = sb("wb_hi", [P, KT, 3 * D], F32R)
        wb_lo = sb("wb_lo", [P, KT, 3 * D], F32R)
        wo = sb("wo", [P, QUADS, D])
        cos = sb("cos", [P, S])
        sin = sb("sin", [P, S])
        bqk = sb("bqk", [P, 4])
        bqk_raw = sb("bqk_raw", [P, 4])
        b1 = sb("b1", [P, FT])
        bv_rows = sb("bv_rows", [P, D])
        bo_rows = sb("bo_rows", [P, D])
        b2_rows = sb("b2_rows", [P, D])
        ident = sb("ident", [P, P])
        gamma = sb("gamma", [P, 2])
        half_gamma = sb("half_gamma", [P, 2, 2])
        abs_sum = sb("abs_sum", [P, 2])
        x = sb("x", [P, TB, D])
        stats = sb("stats", [P, TB, 6])
        mean_var = sb("mean_var", [P, TB, 2])
        rstd = sb("rstd", [P, TB])
        minus_half = sb("minus_half", [P, TB])
        neg_max = sb("neg_max", [P, 4, 2])
        sums = sb("sums", [P, 2, 4 * TB])
        recip = sb("recip", [P, 2, 4 * TB])

        arena = sb("arena", [P, 102 * KB // 4])
        ARENA = nc.lookup_mloc(arena).addr

        def at(name, kb, shape, dt=F32):
            return nc.alloc_sbuf_tensor_at(name, shape, dt, offset=ARENA + kb * KB)

        xh = at("xh", 0, [P, KT, S], F32R)
        xl = at("xl", 4, [P, KT, S], F32R)
        xn = at("xn", 8, [P, TB, D])
        v_a = at("v_a", 12, [P, TB, DA])
        heads_a = at("heads_a", 28, [P, PAIRS, S])
        stack_a = at("stack_a", 44, [P, 2, 2, 3, S], F32R)
        et_a = at("et_a", 68, [P, 4, TB, HS])
        e_a = at("e_a", 84, [P, 2, 2, S])
        raw_a = at("raw_a", 92, [P, 4, S], F32R)
        rs = at("rs", 100, [P, S])
        h32 = at("h32", 12, [P, 2, S])
        h_hi = at("h_hi", 68, [P, FT, S], F32R)
        h_lo = at("h_lo", 84, [P, FT, S], F32R)
        v_b = at("v_b", 12, [P, TB, H, 32])
        k_stack = at("k_stack", 20, [P, H, S], F32R)
        q_stack = at("q_stack", 52, [P, PAIRS, S], F32R)
        qk_flat = at("qk_flat", 68, [P, 4, S])
        rope_hl = at("rope_hl", 76, [P, 2, 2, 2, S], F32R)
        rot = at("rot", 92, [P, 4, S])
        et_b = at("et_b", 68, [P, 6, TB, HS])
        e_b = at("e_b", 92, [P, 2, 2, S])
        heads_b = at("heads_b", 0, [P, QUADS, S])
        wa_raw = at("wa_raw", 0, [P, KT, 3 * DA])
        w1_raw = at("w1_raw", 24, [P, KT, FF])
        w2_raw = at("w2_raw", 32, [P, FT, D])
        wb_raw = at("wb_raw", 40, [P, KT, 3 * D])
        below = at("below", 46, [P, KT * FF])
        ones = at("ones", 54, [P, P])

        def ps(name, shape):
            return ctx.enter_context(nc.psum_tensor(name, shape, F32))

        ps_s = ps("ps_s", [P, 4, S])
        ps_t = ps("ps_t", [P, 2, S])
        ps_o = ps("ps_o", [P, S])
        ps_m = ps("ps_m", [P, S])

        ids = []

        def sem(name):
            h = ctx.enter_context(nc.semaphore(name))
            ids.append(h.num)
            return h

        weights_in = sem("weights_in")
        consts_set = sem("consts_set")
        abs_summed = sem("abs_summed")
        gamma_summed = sem("gamma_summed")
        dve_step = sem("dve_step")
        x_in = sem("x_in")
        x_out = sem("x_out")
        var_ready = sem("var_ready")
        rstd_ready = sem("rstd_ready")
        xn_ready = sem("xn_ready")
        xt_ready = sem("xt_ready")
        xh_ready = sem("xh_ready")
        xl_ready = sem("xl_ready")
        va_proj = sem("va_proj")
        va_even = sem("va_even")
        va_odd = sem("va_odd")
        proj_ready = sem("proj_ready")
        hi_ready = sem("hi_ready")
        lo_ready = sem("lo_ready")
        stacked = [sem("stacked0"), sem("stacked1")]
        qk_done = sem("qk_done")
        max_done = sem("max_done")
        exp_done = sem("exp_done")
        tr_done = sem("tr_done")
        et_act = sem("et_act")
        et_dve = sem("et_dve")
        av_done = sem("av_done")
        recip_ready = sem("recip_ready")
        rows_ready = sem("rows_ready")
        rs_ready = sem("rs_ready")
        normed = sem("normed")
        gelu_done = sem("gelu_done")
        post_done = sem("post_done")
        h_proj = sem("h_proj")
        relu_done = sem("relu_done")
        h_split = sem("h_split")
        y_done = sem("y_done")
        cleared = sem("cleared")
        bqk_proj = sem("bqk_proj")
        bqk_flat_ready = sem("bqk_flat_ready")
        vb_proj = sem("vb_proj")
        vb_ready = sem("vb_ready")
        roped = sem("roped")
        b_stacked = sem("b_stacked")
        wo_done = sem("wo_done")
        result = sem("result")
        every_sem = range(min(ids), max(ids) + 1)

        with nc.Block() as block:
            @block.sync
            def _(sp):
                for i, w in enumerate((WQ, WK, WV)):
                    sp.dma_start(wa_raw[:, :, i * DA:(i + 1) * DA],
                                 w.rearrange("(k p) n -> p k n", p=P)).then_inc(weights_in, 16)
                sp.dma_start(w1_raw[:, :, :], W1T.rearrange("(k p) n -> p k n", p=P)).then_inc(weights_in, 16)
                sp.dma_start(w2_raw[:, :, :], W2T.rearrange("(k p) n -> p k n", p=P)).then_inc(weights_in, 16)
                sp.dma_start(wb_raw[:, :, :], WB.rearrange("(k p) n -> p k n", p=P)).then_inc(weights_in, 16)
                sp.dma_start(wpost[:, :, :], WPOST.rearrange("(k p) n -> p k n", p=P)).then_inc(weights_in, 16)
                sp.dma_start(cos[:, :], COS).then_inc(weights_in, 16)
                sp.dma_start(sin[:, :], SIN).then_inc(weights_in, 16)
                sp.dma_start(bqk_raw[:, :], BQK).then_inc(weights_in, 16)
                sp.dma_start(b1[:, :], B1).then_inc(weights_in, 16)
                for rows, src in ((bv_rows, BV), (bo_rows, BO), (b2_rows, B2)):
                    sp.dma_start(rows[:, :], src.to_broadcast([P, D])).then_inc(weights_in, 16)
                sp.wait_ge(consts_set, 1)
                for j in range(4):
                    sp.dma_start(wo[32 * j:32 * j + HB, :, :], WO[j]).then_inc(weights_in, 16)
                sp.wait_ge(weights_in, 18 * 16)

            @block.gpsimd
            def _(pool):
                nc.gpsimd.memset(wo[:, :, :], 0.0).then_inc(consts_set, 1)
                nc.gpsimd.memset(ones[:, :], 1.0).then_inc(consts_set, 1)
                nc.gpsimd.memset(ident[:, :], 0.0).then_inc(consts_set, 1)
                nc.gpsimd.memset(minus_half[:, :], -0.5).then_inc(consts_set, 1)
                pool.wait_ge(consts_set, 3)
                nc.gpsimd.affine_select(out=ident[:, :], in_=ident[:, :], compare_op=ALU.not_equal, fill=1.0,
                                        base=0, pattern=[[-1, P]], channel_multiplier=1).then_inc(consts_set, 1)

            @block.tensor
            def _(pe):
                pe.wait_ge(consts_set, 2)
                pe.wait_ge(abs_summed, 2)
                nc.tensor.matmul(ps_m[:, 0:2], ones[:, :], abs_sum[:, :], start=True, stop=True).then_inc(gamma_summed, 1)

            @block.vector
            def _(dve):
                steps = [0]

                def link(ins):
                    steps[0] += 1
                    ins.then_inc(dve_step, 1)
                    dve.wait_ge(dve_step, steps[0])

                dve.wait_ge(weights_in, 18 * 16)
                nc.vector.tensor_reduce(abs_sum[:, 0:1], w1_raw[:, :, :].rearrange("p k n -> p (k n)"), AX.X, ALU.add,
                                        apply_absolute_value=True).then_inc(abs_summed, 1)
                nc.vector.tensor_reduce(abs_sum[:, 1:2], w2_raw[:, :, :].rearrange("p k n -> p (k n)"), AX.X, ALU.add,
                                        apply_absolute_value=True).then_inc(abs_summed, 1)
                link(nc.vector.tensor_copy(wa_hi[:, :, :], wa_raw[:, :, :]))
                nc.vector.tensor_tensor(wa_lo[:, :, :], wa_raw[:, :, :], wa_hi[:, :, :], ALU.subtract)
                link(nc.vector.tensor_copy(wb_hi[:, :, :], wb_raw[:, :, :]))
                nc.vector.tensor_tensor(wb_lo[:, :, :], wb_raw[:, :, :], wb_hi[:, :, :], ALU.subtract)
                nc.vector.tensor_scalar(bqk[:, 0:2], bqk_raw[:, 0:2], SCALE_B, None, ALU.mult)
                nc.vector.tensor_copy(bqk[:, 2:4], bqk_raw[:, 2:4])
                dve.wait_ge(gamma_summed, 1)
                link(nc.vector.tensor_scalar(gamma[:, :], ps_m[:, 0:2], 1.0 / (D * FF), EPS, ALU.mult, ALU.add))
                link(nc.vector.tensor_scalar(half_gamma[:, 0, :], gamma[:, :], 0.5, None, ALU.mult))
                link(nc.vector.tensor_scalar(half_gamma[:, 1, :], gamma[:, :], -0.5, None, ALU.mult))
                for i, (raw, w) in enumerate(((w1_raw, w1), (w2_raw, w2))):
                    flat = raw[:, :, :].rearrange("p k n -> p (k n)")
                    link(nc.vector.tensor_scalar(below[:, :], flat, half_gamma[:, 1, i:i + 1], None, ALU.is_lt))
                    link(nc.vector.scalar_tensor_tensor(w[:, :, :].rearrange("p k n -> p (k n)"), flat,
                                                        half_gamma[:, 0, i:i + 1], below[:, :],
                                                        ALU.is_gt, ALU.subtract))

        nc.all_engine_barrier(sems_to_clear=every_sem)

        with nc.Fori(0, BATCH) as b:
            with nc.Block() as block:

                @block.sync
                def _(sp):
                    sp.dma_start(x[:, :, :], X[b, :, :].rearrange("(t p) d -> p t d", p=P)).then_inc(x_in, 16)
                    for p in range(PAIRS):
                        sp.wait_ge(lo_ready, 2 * p + 2)
                        if p >= 2:
                            sp.wait_ge(qk_done, 4 * (p - 1))
                        for h in range(2):
                            src = slice(HA * h, HA * (h + 1))
                            dst = stack_a[:, p % 2, h, :, :].bitcast(F32)
                            raw = raw_a[:, :, :].bitcast(F32)
                            sp.dma_start(dst[0:HA, 0, :], raw[src, 0, :]).then_inc(stacked[p % 2], 16)
                            sp.dma_start(dst[0:HA, 1:3, :], raw[src, 2:4, :]).then_inc(stacked[p % 2], 16)
                            sp.dma_start(dst[HA:P, :, :], raw[src, 1:4, :]).then_inc(stacked[p % 2], 16)
                    sp.wait_ge(cleared, 2)
                    sp.wait_ge(roped, 2)
                    for h in range(H):
                        lanes = slice(8 * h, 8 * h + 8)
                        r0 = 64 * (h % 2)
                        for part in range(2):
                            rows = slice(r0 + 32 * part, r0 + 32 * part + 32)
                            sp.dma_start(k_stack[rows, h, :].bitcast(F32), rope_hl[lanes, 1, :, :, :].bitcast(F32))\
                                .then_inc(b_stacked, 16)
                            for twice in range(2):
                                rows = slice(r0 + 32 * part + twice, r0 + 32 * part + twice + 31, 2)
                                sp.dma_start(q_stack[rows, h // 2, :].bitcast(F32), rope_hl[lanes, 0, :, part, :].bitcast(F32))\
                                    .then_inc(b_stacked, 16)
                    sp.wait_ge(result, TB)
                    sp.dma_start(OUT[b, :, :].rearrange("(t p) d -> p t d", p=P), x[:, :, :]).then_inc(x_out, 16)
                    sp.wait_ge(x_out, 16)

                @block.gpsimd
                def _(pool):
                    def inverse_deviation(n):
                        pool.wait_ge(var_ready, n + 1)
                        nc.gpsimd.tensor_tensor(rstd[:, :], rstd[:, :], minus_half[:, :], ALU.pow).then_inc(rstd_ready, 1)

                    inverse_deviation(0)
                    inverse_deviation(1)
                    pool.wait_ge(post_done, TB)
                    nc.gpsimd.memset(k_stack[:, :, :].bitcast(F32), 0.0).then_inc(cleared, 1)
                    nc.gpsimd.memset(q_stack[:, :, :].bitcast(F32), 0.0).then_inc(cleared, 1)
                    inverse_deviation(2)
                    pool.wait_ge(y_done, TB)
                    nc.gpsimd.memset(v_b[:, :, :, :], 0.0).then_inc(cleared, 1)
                    inverse_deviation(3)

                @block.tensor
                def _(pe):
                    mm, tr = nc.tensor.matmul, nc.tensor.transpose

                    def transpose_x(n):
                        for k in range(KT):
                            for t in range(TB):
                                if k == 0:
                                    pe.wait_ge(xn_ready, TB * n + t + 1)
                                last = tr(ps_t[:, k, t * P:(t + 1) * P], xn[:, t, k * P:(k + 1) * P], ident[:, :])
                            last.then_inc(xt_ready, 1)
                        pe.wait_ge(xl_ready, KT * (n + 1))

                    def passes(hi, lo):
                        for k in range(KT):
                            yield k, xh, hi
                            yield k, xh, lo
                        for k in range(KT):
                            yield k, xl, hi

                    def feature_major(out, hi, lo, c0):
                        todo = list(passes(hi, lo))
                        for i, (k, xs, w) in enumerate(todo):
                            last = mm(out, w[:, k, c0:c0 + P], xs[:, k, :], start=(i == 0), stop=(i == len(todo) - 1))
                        return last

                    def token_major(out, hi, lo, t, c0, n):
                        todo = list(passes(hi, lo))
                        for i, (k, xs, w) in enumerate(todo):
                            last = mm(out, xs[:, k, t * P:(t + 1) * P], w[:, k, c0:c0 + n],
                                      start=(i == 0), stop=(i == len(todo) - 1))
                        return last

                    def transposes(u, e):
                        pe.wait_ge(exp_done, u + 1)
                        for t in range(TB):
                            for j in range(2):
                                c = (t % 2) * HS + j * P
                                last = tr(ps_t[:, t // 2, c:c + P], e[:, u % 2, j, t * P:(t + 1) * P], ident[:, :])
                        last.then_inc(tr_done, 1)

                    transpose_x(0)
                    for g in range(2 * TB):
                        if g >= 4:
                            pe.wait_ge((va_even, va_odd)[g % 2], (g - 4) // 2 + 1)
                        token_major(ps_s[:, g % 4, :], wa_hi, wa_lo, g // 2, 2 * DA + (g % 2) * S, S).then_inc(va_proj, 1)

                    def project(p, i):
                        if p or i:
                            pe.wait_ge(lo_ready, 2 * p + i)
                        if p >= 3:
                            pe.wait_ge(rs_ready, p - 2)
                        feature_major(ps_m[:, :], wa_hi, wa_lo, i * DA + p * P).then_inc(proj_ready, 1)

                    def scores_a(u):
                        p, half, h = u // 4, (u // 2) % 2, u % 2
                        if u % 4 == 0:
                            pe.wait_ge(stacked[p % 2], 6 * 16 * (p // 2 + 1))
                        if u >= 2:
                            pe.wait_ge(exp_done, u - 1)
                        st = stack_a[:, p % 2, h, :, :]
                        for j in range(2):
                            c = (2 * half + j) * P
                            out = ps_s[:, 2 * (u % 2) + j, :]
                            mm(out, st[:, 0, c:c + P], st[:, 1, :], start=True, stop=False)
                            last = mm(out, st[:, 0, c:c + P], st[:, 2, :], start=False, stop=True)
                        last.then_inc(qk_done, 1)

                    def values_a(n):
                        p, half = n // 2, n % 2
                        pe.wait_ge(et_act, 2 * n + 2)
                        pe.wait_ge(et_dve, 2 * n + 2)
                        if half == 0 and p >= 1:
                            pe.wait_ge(normed, p)
                        for t in range(TB):
                            for h in range(2):
                                c = (2 * p + h) * HA
                                last = mm(ps_o[HA * h:HA * (h + 1), half * HS:(half + 1) * HS], v_a[:, t, c:c + HA],
                                          et_a[:, (2 * n + h) % 4, t, :], start=(t == 0), stop=(t == TB - 1))
                        last.then_inc(av_done, 1)

                    def reciprocal_rows(n, group, width):
                        pe.wait_ge(recip_ready, n + 1)
                        if n:
                            pe.wait_ge(rs_ready, n)
                        for t in range(TB):
                            for h in range(group):
                                r = recip[:, n % 2, h * TB + t:h * TB + t + 1].to_broadcast([P, width])
                                last = mm(ps_m[width * h:width * (h + 1), t * P:(t + 1) * P], r, ident[:, :],
                                          start=True, stop=True)
                        last.then_inc(rows_ready, 1)

                    for p in range(2):
                        project(p, 0)
                        project(p, 1)
                    pe.wait_ge(va_even, TB)
                    pe.wait_ge(va_odd, TB)
                    scores_a(0)
                    scores_a(1)
                    for u in range(UNITS):
                        p, r = u // 4, u % 4
                        if u + 2 < UNITS:
                            scores_a(u + 2)
                        if r == 0 and p:
                            values_a(2 * p - 1)
                            pe.wait_ge(lo_ready, 2 * min(p + 1, PAIRS - 1) + 2)
                            reciprocal_rows(p - 1, 2, HA)
                        if r == 2:
                            values_a(2 * p)
                        if u >= 1:
                            pe.wait_ge(et_act, u)
                            pe.wait_ge(et_dve, u)
                        transposes(u, e_a)
                        if r >= 2 and p + 2 < PAIRS:
                            project(p + 2, r - 2)
                    values_a(2 * PAIRS - 1)
                    reciprocal_rows(PAIRS - 1, 2, HA)

                    for k in range(DA // P):
                        if k % 2 == 0:
                            pe.wait_ge(gelu_done, k // 2 + 1)
                        for t in range(TB):
                            last = mm(ps_s[:, t, 0:D], heads_a[:, k, t * P:(t + 1) * P], wpost[:, k, :],
                                      start=(k == 0), stop=(k == DA // P - 1))
                            if k == DA // P - 1:
                                last.then_inc(post_done, 1)

                    y_banks = [ps_t[:, 0, :], ps_t[:, 1, :], ps_o[:, :], ps_m[:, :]]

                    def ffn(n):
                        transpose_x(1 + 2 * n)

                        def up(f):
                            if f >= 4:
                                pe.wait_ge(relu_done, FT * n + f - 3)
                            todo = [(k, xs) for xs in (xh, xl) for k in range(KT)]
                            for i, (k, xs) in enumerate(todo):
                                last = mm(ps_s[:, f % 4, :], w1[:, k, f * P:(f + 1) * P], xs[:, k, :],
                                          start=(i == 0), stop=(i == len(todo) - 1))
                            last.then_inc(h_proj, 1)

                        for f in range(3):
                            up(f)
                        for f in range(FT):
                            if f + 3 < FT:
                                up(f + 3)
                            pe.wait_ge(h_split, FT * n + f + 1)
                            for t in range(TB):
                                for i, part in enumerate((h_hi, h_lo)):
                                    last = mm(y_banks[t][:, 0:D], part[:, f, t * P:(t + 1) * P], w2[:, f, :],
                                              start=(f == 0 and i == 0), stop=(f == FT - 1 and i == 1))
                                if f == FT - 1:
                                    last.then_inc(y_done, 1)

                    ffn(0)

                    transpose_x(2)
                    for j in range(4):
                        feature_major(ps_s[:, j, :], wb_hi, wb_lo, j * P).then_inc(bqk_proj, 1)
                    for t in range(TB):
                        token_major(y_banks[t][:, 0:D], wb_hi, wb_lo, t, 2 * D, D).then_inc(vb_proj, 1)

                    def scores_b(u):
                        half, h = (u // 4) % 2, 4 * (u // 8) + u % 4
                        if u >= 2:
                            pe.wait_ge(exp_done, UNITS + u - 1)
                        for j in range(2):
                            c = (2 * half + j) * P
                            last = mm(ps_s[:, 2 * (u % 2) + j, :], q_stack[:, h // 2, c:c + P], k_stack[:, h, :],
                                      start=True, stop=True)
                        last.then_inc(qk_done, 1)

                    def values_b(n):
                        quad, half = n // 2, n % 2
                        pe.wait_ge(et_act, UNITS + 4 * n + 4)
                        pe.wait_ge(et_dve, UNITS + 4 * n + 4)
                        if half == 0 and quad >= 1:
                            pe.wait_ge(normed, PAIRS + quad)
                        for t in range(TB):
                            for h in range(4):
                                last = mm(ps_o[32 * h:32 * (h + 1), half * HS:(half + 1) * HS], v_b[:, t, 4 * quad + h, :],
                                          et_b[:, (4 * n + h) % 6, t, :], start=(t == 0), stop=(t == TB - 1))
                        last.then_inc(av_done, 1)

                    pe.wait_ge(b_stacked, 6 * H * 16)
                    pe.wait_ge(vb_ready, TB)
                    scores_b(0)
                    scores_b(1)
                    for u in range(UNITS):
                        if u + 2 < UNITS:
                            scores_b(u + 2)
                        if u % 4 == 0 and u:
                            values_b(u // 4 - 1)
                        if u % 8 == 0 and u:
                            reciprocal_rows(PAIRS + u // 8 - 1, 4, 32)
                        if u >= 1:
                            pe.wait_ge(et_act, UNITS + u)
                            pe.wait_ge(et_dve, UNITS + u)
                        transposes(UNITS + u, e_b)
                    values_b(2 * QUADS - 1)
                    reciprocal_rows(PAIRS + QUADS - 1, 4, 32)
                    for g in range(QUADS):
                        pe.wait_ge(normed, PAIRS + g + 1)
                        for t in range(TB):
                            last = mm(ps_s[:, t, 0:D], heads_b[:, g, t * P:(t + 1) * P], wo[:, g, :],
                                      start=(g == 0), stop=(g == QUADS - 1))
                            if g == QUADS - 1:
                                last.then_inc(wo_done, 1)

                    ffn(1)

                @block.scalar
                def _(act):
                    def x_high(n):
                        for k in range(KT):
                            act.wait_ge(xt_ready, KT * n + k + 1)
                            nc.scalar.activation(xh[:, k, :], ps_t[:, k, :], ACT.Copy).then_inc(xh_ready, 1)

                    def exps(u, e, n, i):
                        act.wait_ge(max_done, u + 1)
                        if u >= 2:
                            act.wait_ge(tr_done, u - 1)
                        for j in range(2):
                            ins = nc.scalar.activation(e[:, u % 2, j, :], ps_s[:, 2 * (u % 2) + j, :], ACT.Exp,
                                                       bias=neg_max[:, u % 4, j:j + 1],
                                                       accum_out=sums[:, n % 2, i + j:i + j + 1])
                        ins.then_inc(exp_done, 1)

                    def evacuate(u, et):
                        act.wait_ge(tr_done, u + 1)
                        nc.scalar.activation(et[:, 2:4, :].rearrange("p t s -> p (t s)"), ps_t[:, 1, :], ACT.Copy)\
                            .then_inc(et_act, 1)

                    def rows(n):
                        act.wait_ge(rows_ready, n + 1)
                        if n >= 1:
                            act.wait_ge(normed, n)
                        nc.scalar.activation(rs[:, :], ps_m[:, :], ACT.Copy).then_inc(rs_ready, 1)

                    x_high(0)
                    for g in range(0, 2 * TB, 2):
                        act.wait_ge(va_proj, g + 1)
                        nc.scalar.activation(v_a[:, g // 2, 0:S], ps_s[:, g % 4, :], ACT.Copy).then_inc(va_even, 1)

                    def high(p, i):
                        act.wait_ge(proj_ready, 2 * p + i + 1)
                        if i == 0 and p >= 1:
                            act.wait_ge(stacked[(p - 1) % 2], 6 * 16 * ((p - 1) // 2 + 1))
                        nc.scalar.activation(raw_a[:, 2 * i, :], ps_m[:, :], ACT.Copy,
                                             scale=SCALE_A if i == 0 else 1.0).then_inc(hi_ready, 1)

                    def exps_a(u):
                        exps(u, e_a, u // 4, (u % 2) * TB + (u // 2) % 2 * 2)

                    for p in range(2):
                        high(p, 0)
                        high(p, 1)
                    exps_a(0)
                    for u in range(UNITS):
                        p, r = u // 4, u % 4
                        if u + 1 < UNITS:
                            exps_a(u + 1)
                        if r == 0 and p:
                            rows(p - 1)
                        if u >= 4:
                            act.wait_ge(av_done, (u - 4) // 2 + 1)
                        evacuate(u, et_a[:, u % 4, :, :])
                        if r >= 2 and p + 2 < PAIRS:
                            high(p + 2, r - 2)
                    rows(PAIRS - 1)
                    for c in range(DA // P // 2):
                        act.wait_ge(normed, 2 * c + 2)
                        tile = heads_a[:, 2 * c:2 * c + 2, :].rearrange("p k s -> p (k s)")
                        nc.scalar.activation(tile, tile, ACT.Gelu).then_inc(gelu_done, 1)

                    def ffn(n):
                        x_high(1 + 2 * n)
                        for f in range(FT):
                            act.wait_ge(h_proj, FT * n + f + 1)
                            if n or f >= 2:
                                act.wait_ge(h_split, FT * n + f - 1)
                            nc.scalar.activation(h32[:, f % 2, :], ps_s[:, f % 4, :], ACT.Relu,
                                                 bias=b1[:, f:f + 1]).then_inc(relu_done, 1)

                    ffn(0)

                    x_high(2)
                    for j in range(4):
                        act.wait_ge(bqk_proj, j + 1)
                        nc.scalar.activation(qk_flat[:, j, :], ps_s[:, j, :], ACT.Identity, bias=bqk[:, j:j + 1],
                                             scale=SCALE_B if j < 2 else 1.0).then_inc(bqk_flat_ready, 1)

                    def exps_b(u):
                        exps(UNITS + u, e_b, PAIRS + u // 8, (u % 4) * TB + (u // 4) % 2 * 2)

                    exps_b(0)
                    for u in range(UNITS):
                        if u + 1 < UNITS:
                            exps_b(u + 1)
                        if u % 8 == 0 and u:
                            rows(PAIRS + u // 8 - 1)
                        if u >= 6:
                            act.wait_ge(av_done, 2 * PAIRS + (u - 6) // 4 + 1)
                        evacuate(UNITS + u, et_b[:, u % 6, :, :])
                    rows(PAIRS + QUADS - 1)

                    ffn(1)

                @block.vector
                def _(dve):
                    steps = [0]

                    def link(ins):
                        steps[0] += 1
                        ins.then_inc(dve_step, 1)
                        dve.wait_ge(dve_step, steps[0])

                    def layernorm(n):
                        for t in range(TB):
                            ins = nc.vector.bn_stats(stats[:, t, :], x[:, t, :])
                        link(ins)
                        for t in range(TB):
                            ins = nc.vector.bn_aggr(mean_var[:, t, :], stats[:, t, :])
                        link(ins)
                        nc.vector.tensor_scalar(rstd[:, :], mean_var[:, :, 1], EPS, None, ALU.add).then_inc(var_ready, 1)
                        dve.wait_ge(rstd_ready, n + 1)
                        for t in range(TB):
                            nc.vector.tensor_scalar(xn[:, t, :], x[:, t, :], mean_var[:, t, 0:1], rstd[:, t:t + 1],
                                                    ALU.subtract, ALU.mult).then_inc(xn_ready, 1)
                        dve.wait_ge(xn_ready, TB * (n + 1))

                    def x_low(n):
                        for k in range(KT):
                            dve.wait_ge(xh_ready, KT * n + k + 1)
                            nc.vector.tensor_tensor(xl[:, k, :], ps_t[:, k, :], xh[:, k, :], ALU.subtract)\
                                .then_inc(xl_ready, 1)

                    def unit_max(u):
                        dve.wait_ge(qk_done, u + 1)
                        nc.vector.reduce_max(neg_max[:, u % 4, :], ps_s[:, 2 * (u % 2):2 * (u % 2) + 2, :], AX.X, negate=True)\
                            .then_inc(max_done, 1)

                    def invert(n, group):
                        nc.vector.reciprocal(recip[:, n % 2, 0:group * TB], sums[:, n % 2, 0:group * TB]).then_inc(recip_ready, 1)

                    dve.wait_ge(x_in, 16)
                    layernorm(0)
                    link(nc.vector.tensor_tensor(x[:, :, :], x[:, :, :], xn[:, :, :], ALU.add))
                    x_low(0)
                    for g in range(1, 2 * TB, 2):
                        dve.wait_ge(va_proj, g + 1)
                        nc.vector.tensor_copy(v_a[:, g // 2, S:DA], ps_s[:, g % 4, :]).then_inc(va_odd, 1)

                    def low(p, i):
                        dve.wait_ge(hi_ready, 2 * p + i + 1)
                        nc.vector.scalar_tensor_tensor(raw_a[:, 2 * i + 1, :], ps_m[:, :], SCALE_A if i == 0 else 1.0,
                                                       raw_a[:, 2 * i, :], ALU.mult, ALU.subtract).then_inc(lo_ready, 1)

                    def norm_a(p):
                        dve.wait_ge(rs_ready, p + 1)
                        dve.wait_ge(av_done, 2 * p + 2)
                        nc.vector.tensor_tensor(heads_a[:, p, :], ps_o[:, :], rs[:, :], ALU.mult).then_inc(normed, 1)

                    for p in range(2):
                        low(p, 0)
                        low(p, 1)
                    unit_max(0)
                    unit_max(1)
                    for u in range(UNITS):
                        p, r = u // 4, u % 4
                        if r == 0 and p:
                            dve.wait_ge(exp_done, 4 * p)
                            invert(p - 1, 2)
                        if u + 2 < UNITS:
                            unit_max(u + 2)
                        if u >= 4:
                            dve.wait_ge(av_done, (u - 4) // 2 + 1)
                        dve.wait_ge(tr_done, u + 1)
                        nc.vector.tensor_copy(et_a[:, u % 4, 0:2, :].rearrange("p t s -> p (t s)"), ps_t[:, 0, :])\
                            .then_inc(et_dve, 1)
                        if r == 0 and p:
                            norm_a(p - 1)
                        if r >= 2 and p + 2 < PAIRS:
                            low(p + 2, r - 2)
                    dve.wait_ge(exp_done, UNITS)
                    invert(PAIRS - 1, 2)
                    norm_a(PAIRS - 1)
                    for t in range(TB):
                        dve.wait_ge(post_done, t + 1)
                        ins = nc.vector.tensor_tensor(x[:, t, :], x[:, t, :], ps_s[:, t, 0:D], ALU.add)
                    link(ins)

                    y_banks = [ps_t[:, 0, :], ps_t[:, 1, :], ps_o[:, :], ps_m[:, :]]

                    def ffn(n):
                        layernorm(1 + 2 * n)
                        link(nc.vector.tensor_tensor(x[:, :, :], x[:, :, :], rows_of(b2_rows), ALU.add))
                        x_low(1 + 2 * n)
                        for f in range(FT):
                            dve.wait_ge(relu_done, FT * n + f + 1)
                            link(nc.vector.tensor_copy(h_hi[:, f, :], h32[:, f % 2, :]))
                            nc.vector.tensor_tensor(h_lo[:, f, :], h32[:, f % 2, :], h_hi[:, f, :], ALU.subtract)\
                                .then_inc(h_split, 1)
                        for t in range(TB):
                            dve.wait_ge(y_done, TB * n + t + 1)
                            ins = nc.vector.tensor_tensor(x[:, t, :], x[:, t, :], y_banks[t][:, 0:D], ALU.add)
                            if n:
                                ins.then_inc(result, 1)
                        if not n:
                            link(ins)

                    def rows_of(tile):
                        return tile[:, :].rearrange("p (o d) -> p o d", o=1).to_broadcast([P, TB, D])

                    ffn(0)

                    layernorm(2)
                    link(nc.vector.tensor_tensor(x[:, :, :], x[:, :, :], rows_of(bo_rows), ALU.add))
                    x_low(2)
                    for i in range(2):
                        dve.wait_ge(bqk_flat_ready, 2 * i + 2)
                        a, c = qk_flat[:, 2 * i, :], qk_flat[:, 2 * i + 1, :]
                        nc.vector.tensor_tensor(rot[:, 0, :], a, cos[:, :], ALU.mult)
                        nc.vector.tensor_tensor(rot[:, 1, :], c, sin[:, :], ALU.mult)
                        nc.vector.tensor_tensor(rot[:, 2, :], a, sin[:, :], ALU.mult)
                        link(nc.vector.tensor_tensor(rot[:, 3, :], c, cos[:, :], ALU.mult))
                        nc.vector.tensor_tensor(rot[:, 0, :], rot[:, 0, :], rot[:, 1, :], ALU.subtract)
                        link(nc.vector.tensor_tensor(rot[:, 2, :], rot[:, 2, :], rot[:, 3, :], ALU.add))
                        link(nc.vector.tensor_copy(rope_hl[:, i, :, 0, :], rot[:, 0:3:2, :]))
                        nc.vector.tensor_tensor(rope_hl[:, i, :, 1, :], rot[:, 0:3:2, :], rope_hl[:, i, :, 0, :],
                                                ALU.subtract).then_inc(roped, 1)
                        dve.wait_ge(roped, i + 1)
                    dve.wait_ge(cleared, 3)
                    for t in range(TB):
                        dve.wait_ge(vb_proj, t + 1)
                        nc.vector.tensor_tensor(v_b[:, t, :, 0:HB],
                                                y_banks[t][:, 0:D].rearrange("p (h d) -> p h d", d=HB),
                                                bv_rows[:, :].rearrange("p (h d) -> p h d", d=HB), ALU.add)\
                            .then_inc(vb_ready, 1)

                    def norm_b(g):
                        dve.wait_ge(rs_ready, PAIRS + g + 1)
                        dve.wait_ge(av_done, 2 * PAIRS + 2 * g + 2)
                        nc.vector.tensor_tensor(heads_b[:, g, :], ps_o[:, :], rs[:, :], ALU.mult).then_inc(normed, 1)

                    unit_max(UNITS)
                    unit_max(UNITS + 1)
                    for u in range(UNITS):
                        if u % 8 == 0 and u:
                            dve.wait_ge(exp_done, UNITS + u)
                            invert(PAIRS + u // 8 - 1, 4)
                        if u + 2 < UNITS:
                            unit_max(UNITS + u + 2)
                        if u >= 6:
                            dve.wait_ge(av_done, 2 * PAIRS + (u - 6) // 4 + 1)
                        dve.wait_ge(tr_done, UNITS + u + 1)
                        nc.vector.tensor_copy(et_b[:, u % 6, 0:2, :].rearrange("p t s -> p (t s)"), ps_t[:, 0, :])\
                            .then_inc(et_dve, 1)
                        if u % 8 == 0 and u:
                            norm_b(u // 8 - 1)
                    dve.wait_ge(exp_done, 2 * UNITS)
                    invert(PAIRS + QUADS - 1, 4)
                    norm_b(QUADS - 1)
                    for t in range(TB):
                        dve.wait_ge(wo_done, t + 1)
                        ins = nc.vector.tensor_tensor(x[:, t, :], x[:, t, :], ps_s[:, t, 0:D], ALU.add)
                    link(ins)

                    ffn(1)

            nc.all_engine_barrier(sems_to_clear=every_sem)


def kernel(**inputs):
    import numpy as np
    import concourse.bacc as bacc
    from concourse.bass_utils import run_bass_kernel_spmd

    def get(name):
        return np.asarray(inputs["L0_" + name])

    half, tokens = 8, 512
    pos = np.arange(tokens, dtype=np.float32)[:, None]
    freq = np.float32(1.0) / np.float32(10000.0) ** (np.arange(half, dtype=np.float32) / np.float32(half))
    angles = (pos * freq[None, :]).astype(np.float32)
    cos = np.ascontiguousarray(np.tile(np.cos(angles).astype(np.float32).T, (16, 1)))
    sin = np.ascontiguousarray(np.tile(np.sin(angles).astype(np.float32).T, (16, 1)))

    def halves(w):
        lead = w.shape[:-1]
        return np.swapaxes(w.reshape(*lead, 16, 2, 8), -3, -2).reshape(*lead, 256)

    wb = np.concatenate([halves(get("attn_b_wq_w")), halves(get("attn_b_wk_w")), get("attn_b_wv_w")], axis=1)
    bqk = np.concatenate([halves(get("attn_b_wq_b")), halves(get("attn_b_wk_b"))]).reshape(4, 128).T
    wo = get("attn_b_wo_w").reshape(4, 4, 16, 256).transpose(1, 2, 0, 3)
    arrays = {
        "X": get("attn_a_X"), "WQ": get("attn_a_Wq"), "WK": get("attn_a_Wk"), "WV": get("attn_a_Wv"),
        "WPOST": get("attn_a_Wpost"), "WB": wb, "BQK": bqk, "BV": get("attn_b_wv_b").reshape(1, 256), "WO": wo,
        "BO": get("attn_b_wo_b").reshape(1, 256), "W1T": get("ffn_W1").T, "B1": get("ffn_b1").reshape(8, 128).T,
        "W2T": get("ffn_W2").T, "B2": get("ffn_b2").reshape(1, 256), "COS": cos, "SIN": sin,
    }
    arrays = {name: np.ascontiguousarray(a) for name, a in arrays.items()}
    nc = bacc.Bacc("TRN2", target_bir_lowering=False, num_devices=1)
    args = [nc.dram_tensor(name, a.shape, mybir.dt.from_np(a.dtype), kind="ExternalInput").ap()
            for name, a in arrays.items()]
    out = nc.dram_tensor("OUT", arrays["X"].shape, mybir.dt.float32, kind="ExternalOutput").ap()
    hybrid_block_kernel(nc, *args, out)
    r = run_bass_kernel_spmd(nc, [arrays], core_ids=[0])
    return r.results[0]["OUT"]
```

```python
import concourse.bass as bass
from concourse import mybir
from contextlib import ExitStack



def hybrid_block_kernel(nc, X, WQ, WK, WV, WPOST, WB, BQK, BV, WO, BO, W1T, B1, W2T, B2, COS, SIN, X1, OUT):
    F32, F32R = mybir.dt.float32, mybir.dt.float32r
    ALU = mybir.AluOpType
    ACT = mybir.ActivationFunctionType
    AX = mybir.AxisListType

    P = 128
    BATCH, S, D = X.shape
    TB = S // P
    KT = D // P
    DA = WQ.shape[1]
    H = 16
    HA = DA // H
    HB = D // H
    PAIRS = H // 2
    FF = W1T.shape[1]
    FT = FF // P
    QUADS = H // 4
    EPS = 1e-5
    SCALE_A = float(HA) ** -0.5
    SCALE_B = float(HB) ** -0.5
    UNITS = 2 * H
    HS = S // 2
    KB = 1024

    ctx = ExitStack()
    with ctx:
        arena = ctx.enter_context(nc.sbuf_tensor("arena", [P, 206 * KB // 4], F32))
        ARENA = nc.lookup_mloc(arena).addr
        arena_end = [0]

        def at(name, kb, shape, dt=F32):
            size = 4
            for n in shape[1:]:
                size *= n
            arena_end[0] = max(arena_end[0], kb * KB + size)
            assert arena_end[0] <= 206 * KB
            return nc.alloc_sbuf_tensor_at(name, shape, dt, offset=ARENA + int(kb * KB))

        ident = at("ident", 0, [P, P])
        rstd = at("rstd", 0.5, [P, TB])
        minus_half = at("minus_half", 0.53125, [P, TB])
        stats = at("stats", 0.5625, [P, TB, 6])
        mean_var = at("mean_var", 0.6875, [P, TB, 2])
        neg_max = at("neg_max", 0.75, [P, 4, 2])
        sums = at("sums", 0.8125, [P, 2, 4 * TB])
        recip = at("recip", 1, [P, 2, 4 * TB])
        abs_sum = at("abs_sum", 1.25, [P, 2])
        gamma = at("gamma", 1.28125, [P, 2])
        half_gamma = at("half_gamma", 1.3125, [P, 2, 2])

        wa_hi = at("wa_hi", 2, [P, KT, 3 * DA], F32R)
        wa_lo = at("wa_lo", 26, [P, KT, 3 * DA], F32R)
        wpost = at("wpost", 50, [P, DA // P, D])
        xh_a = at("xh_a", 58, [P, KT, S], F32R)
        xl_a = at("xl_a", 62, [P, KT, S], F32R)
        xn_a = at("xn_a", 66, [P, TB, D])
        x_next = at("x_next", 70, [P, TB, D])
        res = at("res", 74, [P, TB, D])
        v_a = at("v_a", 78, [P, TB, DA])
        heads_a = at("heads_a", 94, [P, PAIRS, S])
        stack_a = at("stack_a", 110, [P, 2, 2, 3, S], F32R)
        et_a = at("et_a", 134, [P, 4, TB, HS])
        e_a = (at("e_a0", 150, [P, 2, S]), at("e_a1", 154, [P, 2, S]))
        raw_a = at("raw_a", 158, [P, 2, 4, S], F32R)
        rs_a = at("rs_a", 174, [P, S])
        wa_raw = at("wa_raw", 78, [P, KT, 3 * DA])

        w1 = at("w1", 2, [P, KT, FF], F32R)
        w2 = at("w2", 10, [P, FT, D], F32R)
        wb_hi = at("wb_hi", 18, [P, KT, 3 * D], F32R)
        wb_lo = at("wb_lo", 24, [P, KT, 3 * D], F32R)
        wo = at("wo", 30, [P, QUADS, D])
        cos = at("cos", 34, [P, S])
        sin = at("sin", 36, [P, S])
        bqk = at("bqk", 38, [P, 4])
        bqk_raw = at("bqk_raw", 38.0625, [P, 4])
        b1 = at("b1", 38.125, [P, FT])
        bv_rows = at("bv_rows", 39, [P, D])
        bo_rows = at("bo_rows", 40, [P, D])
        b2_rows = at("b2_rows", 41, [P, D])
        x = at("x", 42, [P, TB, D])
        xn = at("xn", 46, [P, TB, D])
        xh = at("xh", 50, [P, KT, S], F32R)
        xl = at("xl", 54, [P, KT, S], F32R)
        v_b = at("v_b", 58, [P, TB, H, 32])
        k_stack = at("k_stack", 66, [P, H // 2, S], F32R)
        q_stack = at("q_stack", 82, [P, PAIRS // 2, S], F32R)
        et_b = at("et_b", 90, [P, 6, TB, HS])
        e_b = (at("e_b0", 114, [P, 2, S]), at("e_b1", 118, [P, 2, S]))
        roped_qk = at("roped_qk", 122, [P, 2, 2, 2, 2, S], F32R)
        rs = at("rs", 154, [P, S])
        heads_b = at("heads_b", 156, [P, QUADS, S])
        h_hi = at("h_hi", 164, [P, FT, S], F32R)
        h_lo = at("h_lo", 180, [P, FT, S], F32R)
        h32 = at("h32", 196, [P, 2, S])
        qk_flat = (at("q_flat", 164, [P, 2, S]), at("k_flat", 168, [P, 2, S]))
        rot = at("rot", 172, [P, 4, S])
        w1_raw = at("w1_raw", 114, [P, KT, FF])
        w2_raw = at("w2_raw", 122, [P, FT, D])
        wb_raw = at("wb_raw", 130, [P, KT, 3 * D])
        below = at("below", 136, [P, KT * FF])
        ones = at("ones", 144, [P, P])

        def ps(name, shape):
            return ctx.enter_context(nc.psum_tensor(name, shape, F32))

        ps_s = ps("ps_s", [P, 4, S])
        ps_t = ps("ps_t", [P, 2, S])
        ps_o = ps("ps_o", [P, S])
        ps_m = ps("ps_m", [P, S])
        wide_banks = [ps_t[:, 0, :], ps_t[:, 1, :], ps_o[:, :], ps_m[:, :]]

        ids = []

        def sem(name):
            h = ctx.enter_context(nc.semaphore(name))
            ids.append(h.num)
            return h

        weights_in = sem("weights_in")
        consts_set = sem("consts_set")
        abs_summed = sem("abs_summed")
        gamma_summed = sem("gamma_summed")
        dve_step = sem("dve_step")
        x_in = sem("x_in")
        x_out = sem("x_out")
        var_ready = sem("var_ready")
        rstd_ready = sem("rstd_ready")
        xn_ready = sem("xn_ready")
        xt_ready = sem("xt_ready")
        xh_ready = sem("xh_ready")
        xl_ready = sem("xl_ready")
        va_proj = sem("va_proj")
        va_even = sem("va_even")
        va_odd = sem("va_odd")
        proj_ready = sem("proj_ready")
        hi_ready = sem("hi_ready")
        lo_ready = sem("lo_ready")
        qk_done = sem("qk_done")
        max_done = sem("max_done")
        exp_done = sem("exp_done")
        tr_done = sem("tr_done")
        et_act = sem("et_act")
        et_dve = sem("et_dve")
        av_done = sem("av_done")
        recip_ready = sem("recip_ready")
        rows_ready = sem("rows_ready")
        rs_ready = sem("rs_ready")
        normed = sem("normed")
        gelu_done = sem("gelu_done")
        post_done = sem("post_done")
        x1_ready = sem("x1_ready")
        res_ready = sem("res_ready")
        h_proj = sem("h_proj")
        relu_done = sem("relu_done")
        h_split = sem("h_split")
        y_done = sem("y_done")
        cleared = sem("cleared")
        bqk_proj = sem("bqk_proj")
        bqk_flat_ready = sem("bqk_flat_ready")
        vb_proj = sem("vb_proj")
        vb_ready = sem("vb_ready")
        roped = sem("roped")
        wo_done = sem("wo_done")
        result = sem("result")
        stacked = [sem("stacked0"), sem("stacked1")]
        b_stacked = [sem(f"b_stacked{i}") for i in range(PAIRS)]
        every_sem = range(min(ids), max(ids) + 1)

        def next_block():
            nc.all_engine_barrier(sems_to_clear=every_sem)

        def rows_of(tile):
            return tile[:, :].rearrange("p (o d) -> p o d", o=1).to_broadcast([P, TB, D])

        def passes(xs_hi, xs_lo, hi, lo):
            for k in range(KT):
                yield k, xs_hi, hi
                yield k, xs_hi, lo
            for k in range(KT):
                yield k, xs_lo, hi

        def feature_major(out, xs_hi, xs_lo, hi, lo, c0):
            todo = list(passes(xs_hi, xs_lo, hi, lo))
            for i, (k, xs, w) in enumerate(todo):
                last = nc.tensor.matmul(out, w[:, k, c0:c0 + P], xs[:, k, :], start=(i == 0), stop=(i == len(todo) - 1))
            return last

        def token_major(out, xs_hi, xs_lo, hi, lo, t, c0, n):
            todo = list(passes(xs_hi, xs_lo, hi, lo))
            for i, (k, xs, w) in enumerate(todo):
                last = nc.tensor.matmul(out, xs[:, k, t * P:(t + 1) * P], w[:, k, c0:c0 + n],
                                        start=(i == 0), stop=(i == len(todo) - 1))
            return last

        def unit_transposes(e):
            for t in range(TB):
                for j in range(2):
                    c = (t % 2) * HS + j * P
                    last = nc.tensor.transpose(ps_t[:, t // 2, c:c + P], e[:, j, t * P:(t + 1) * P], ident[:, :])
            return last

        def reciprocal_products(n, group, width):
            for t in range(TB):
                for h in range(group):
                    r = recip[:, n % 2, h * TB + t:h * TB + t + 1].to_broadcast([P, width])
                    last = nc.tensor.matmul(ps_m[width * h:width * (h + 1), t * P:(t + 1) * P], r, ident[:, :],
                                            start=True, stop=True)
            return last

        with nc.Block() as block:

            @block.sync
            def _(sp):
                for i, w in enumerate((WQ, WK, WV)):
                    sp.dma_start(wa_raw[:, :, i * DA:(i + 1) * DA],
                                 w.rearrange("(k p) n -> p k n", p=P)).then_inc(weights_in, 16)
                sp.dma_start(wpost[:, :, :], WPOST.rearrange("(k p) n -> p k n", p=P)).then_inc(weights_in, 16)
                sp.dma_start(x_next[:, :, :], X[0, :, :].rearrange("(t p) d -> p t d", p=P)).then_inc(weights_in, 16)
                sp.wait_ge(weights_in, 5 * 16)

            @block.gpsimd
            def _(pool):
                nc.gpsimd.memset(minus_half[:, :], -0.5)
                nc.gpsimd.memset(ident[:, :], 0.0).then_inc(consts_set, 1)
                pool.wait_ge(consts_set, 1)
                nc.gpsimd.affine_select(out=ident[:, :], in_=ident[:, :], compare_op=ALU.not_equal, fill=1.0,
                                        base=0, pattern=[[-1, P]], channel_multiplier=1).then_inc(consts_set, 1)

            @block.vector
            def _(dve):
                dve.wait_ge(weights_in, 5 * 16)
                nc.vector.tensor_copy(wa_hi[:, :, :], wa_raw[:, :, :]).then_inc(dve_step, 1)
                dve.wait_ge(dve_step, 1)
                nc.vector.tensor_tensor(wa_lo[:, :, :], wa_raw[:, :, :], wa_hi[:, :, :], ALU.subtract)

        next_block()

        def attention_a(seq, before, now, ahead):
            projs = 2 * (PAIRS - 2) if now else 0
            pair_stacks = 6 * 16
            place = (PAIRS - 2) // 2 * pair_stacks if now else 0

            with nc.Block() as block:

                @block.sync
                def _(sp):
                    def stack(p, at_proj):
                        sp.wait_ge(lo_ready, at_proj + 2)
                        raw = raw_a[:, p % 2, :, :].bitcast(F32)
                        for h in range(2):
                            src = slice(HA * h, HA * (h + 1))
                            dst = stack_a[:, p % 2, h, :, :].bitcast(F32)
                            sp.dma_start(dst[0:HA, 0, :], raw[src, 0, :]).then_inc(stacked[p % 2], 16)
                            sp.dma_start(dst[0:HA, 1:3, :], raw[src, 2:4, :]).then_inc(stacked[p % 2], 16)
                            sp.dma_start(dst[HA:P, :, :], raw[src, 1:4, :]).then_inc(stacked[p % 2], 16)

                    if before:
                        sp.wait_ge(x1_ready, TB)
                        sp.dma_start(X1[seq - 1, :, :].rearrange("(t p) d -> p t d", p=P), res[:, :, :]).then_inc(x_out, 16)
                    if now:
                        for p in range(2, PAIRS):
                            sp.wait_ge(qk_done, 4 * (p - 1))
                            stack(p, 2 * (p - 2))
                            if p == 3 and ahead:
                                sp.wait_ge(res_ready, 1)
                                sp.dma_start(x_next[:, :, :], X[seq + 1, :, :].rearrange("(t p) d -> p t d", p=P))\
                                    .then_inc(x_in, 16)
                    if ahead:
                        for p in range(2):
                            if now:
                                sp.wait_ge(qk_done, 4 * (PAIRS - 1 + p))
                            stack(p, projs + 2 * p)
                        for p in range(2):
                            sp.wait_ge(stacked[p], place + pair_stacks)
                    if before:
                        sp.wait_ge(x_out, 16)

                @block.gpsimd
                def _(pool):
                    if now:
                        if before:
                            pool.wait_ge(x_out, 16)
                        nc.gpsimd.tensor_tensor(res[:, :, :], x_next[:, :, :], xn_a[:, :, :], ALU.add).then_inc(res_ready, 1)
                    if ahead:
                        pool.wait_ge(var_ready, 1)
                        nc.gpsimd.tensor_tensor(rstd[:, :], rstd[:, :], minus_half[:, :], ALU.pow).then_inc(rstd_ready, 1)

                @block.tensor
                def _(pe):
                    mm = nc.tensor.matmul

                    def scores(u):
                        p, half, h = u // 4, (u // 2) % 2, u % 2
                        if u % 4 == 0 and p >= 2:
                            pe.wait_ge(stacked[p % 2], (p // 2) * pair_stacks)
                        if u >= 2:
                            pe.wait_ge(exp_done, u - 1)
                        st = stack_a[:, p % 2, h, :, :]
                        for j in range(2):
                            c = (2 * half + j) * P
                            out = ps_s[:, 2 * (u % 2) + j, :]
                            mm(out, st[:, 0, c:c + P], st[:, 1, :], start=True, stop=False)
                            last = mm(out, st[:, 0, c:c + P], st[:, 2, :], start=False, stop=True)
                        last.then_inc(qk_done, 1)

                    def values(n):
                        p, half = n // 2, n % 2
                        pe.wait_ge(et_act, 2 * n + 2)
                        pe.wait_ge(et_dve, 2 * n + 2)
                        if half == 0 and p >= 1:
                            pe.wait_ge(normed, p)
                        if n == 0 and before:
                            pe.wait_ge(x1_ready, TB)
                        for t in range(TB):
                            for h in range(2):
                                c = (2 * p + h) * HA
                                last = mm(ps_o[HA * h:HA * (h + 1), half * HS:(half + 1) * HS], v_a[:, t, c:c + HA],
                                          et_a[:, (2 * n + h) % 4, t, :], start=(t == 0), stop=(t == TB - 1))
                        last.then_inc(av_done, 1)

                    def recip_rows(n):
                        pe.wait_ge(recip_ready, n + 1)
                        reciprocal_products(n, 2, HA).then_inc(rows_ready, 1)

                    def project(p, i):
                        feature_major(ps_m[:, :], xh_a, xl_a, wa_hi, wa_lo, i * DA + p * P).then_inc(proj_ready, 1)

                    def transpose_x(k):
                        if k == 0:
                            pe.wait_ge(xn_ready, TB)
                        for t in range(TB):
                            last = nc.tensor.transpose(ps_m[:, t * P:(t + 1) * P], xn_a[:, t, k * P:(k + 1) * P], ident[:, :])
                        last.then_inc(xt_ready, 1)

                    if now:
                        scores(0)
                        scores(1)
                    if before:
                        for k in range(PAIRS):
                            if k % 2 == 0:
                                pe.wait_ge(gelu_done, k // 2 + 1)
                            for t in range(TB):
                                last = mm(wide_banks[t][:, 0:D], heads_a[:, k, t * P:(t + 1) * P], wpost[:, k, :],
                                          start=(k == 0), stop=(k == PAIRS - 1))
                                if k == PAIRS - 1:
                                    last.then_inc(post_done, 1)
                    if now:
                        for u in range(UNITS):
                            p, r = u // 4, u % 4
                            if u + 2 < UNITS:
                                scores(u + 2)
                            if r == 0 and p:
                                values(2 * p - 1)
                                if p <= PAIRS - 2:
                                    pe.wait_ge(lo_ready, 2 * p)
                                elif ahead:
                                    pe.wait_ge(xl_ready, 1)
                                else:
                                    pe.wait_ge(rs_ready, p - 1)
                                recip_rows(p - 1)
                            if r == 2:
                                values(2 * p)
                            if u >= 1:
                                pe.wait_ge(et_act, u)
                                pe.wait_ge(et_dve, u)
                            elif before:
                                pe.wait_ge(x1_ready, TB)
                            pe.wait_ge(exp_done, u + 1)
                            unit_transposes(e_a[u % 2]).then_inc(tr_done, 1)
                            if r >= 2 and p + 2 < PAIRS:
                                if r == 2 and p:
                                    pe.wait_ge(rs_ready, p)
                                if r == 3:
                                    pe.wait_ge(lo_ready, 2 * p + 1)
                                project(p + 2, r - 2)
                            if ahead and r == 1 and p >= PAIRS - 2:
                                pe.wait_ge(rs_ready, p)
                                transpose_x(p - (PAIRS - 2))
                    if ahead:
                        if not now:
                            transpose_x(0)
                            pe.wait_ge(xl_ready, 1)
                            transpose_x(1)
                        pe.wait_ge(xl_ready, 2)
                        project(0, 0)
                        pe.wait_ge(lo_ready, projs + 1)
                        project(0, 1)
                    if now:
                        values(2 * PAIRS - 1)
                        if ahead:
                            pe.wait_ge(lo_ready, projs + 2)
                        else:
                            pe.wait_ge(rs_ready, PAIRS - 1)
                        recip_rows(PAIRS - 1)
                    if ahead:
                        if now:
                            pe.wait_ge(rs_ready, PAIRS)
                        else:
                            pe.wait_ge(lo_ready, projs + 2)
                        project(1, 0)
                        for g in range(2 * TB):
                            if g == 2:
                                pe.wait_ge(lo_ready, projs + 3)
                                project(1, 1)
                            if g >= 4:
                                pe.wait_ge((va_even, va_odd)[g % 2], (g - 4) // 2 + 1)
                            token_major(ps_s[:, g % 4, :], xh_a, xl_a, wa_hi, wa_lo, g // 2, 2 * DA + (g % 2) * S, S)\
                                .then_inc(va_proj, 1)

                @block.scalar
                def _(act):
                    def exps(u):
                        p, half, h = u // 4, (u // 2) % 2, u % 2
                        act.wait_ge(max_done, u + 1)
                        if u >= 2:
                            act.wait_ge(tr_done, u - 1)
                        for j in range(2):
                            c = h * TB + 2 * half + j
                            ins = nc.scalar.activation(e_a[u % 2][:, j, :], ps_s[:, 2 * (u % 2) + j, :], ACT.Exp,
                                                       bias=neg_max[:, u % 4, j:j + 1], accum_out=sums[:, p % 2, c:c + 1])
                        ins.then_inc(exp_done, 1)

                    def high(p, i, m):
                        act.wait_ge(proj_ready, m + 1)
                        if i == 0 and m >= 4:
                            act.wait_ge(stacked[p % 2], ((m - 4) // 4 + 1) * pair_stacks)
                        nc.scalar.activation(raw_a[:, p % 2, 2 * i, :], ps_m[:, :], ACT.Copy,
                                             scale=SCALE_A if i == 0 else 1.0).then_inc(hi_ready, 1)

                    def x_high(k):
                        act.wait_ge(xt_ready, k + 1)
                        nc.scalar.activation(xh_a[:, k, :], ps_m[:, :], ACT.Copy).then_inc(xh_ready, 1)

                    def rows(n):
                        act.wait_ge(rows_ready, n + 1)
                        if n >= 1:
                            act.wait_ge(normed, n)
                        nc.scalar.activation(rs_a[:, :], ps_m[:, :], ACT.Copy).then_inc(rs_ready, 1)

                    if before:
                        for c in range(PAIRS // 2):
                            tile = heads_a[:, 2 * c:2 * c + 2, :].rearrange("p k s -> p (k s)")
                            nc.scalar.activation(tile, tile, ACT.Gelu).then_inc(gelu_done, 1)
                    if now:
                        exps(0)
                        for u in range(UNITS):
                            p, r = u // 4, u % 4
                            if u + 1 < UNITS:
                                exps(u + 1)
                            if r == 0 and p:
                                rows(p - 1)
                            if u >= 4:
                                act.wait_ge(av_done, (u - 4) // 2 + 1)
                            act.wait_ge(tr_done, u + 1)
                            nc.scalar.activation(et_a[:, u % 4, 2:4, :].rearrange("p t s -> p (t s)"), ps_t[:, 1, :],
                                                 ACT.Copy).then_inc(et_act, 1)
                            if r >= 2 and p + 2 < PAIRS:
                                high(p + 2, r - 2, 2 * p + r - 2)
                            if ahead and r == 1 and p >= PAIRS - 2:
                                x_high(p - (PAIRS - 2))
                    if ahead:
                        if not now:
                            x_high(0)
                            x_high(1)
                        high(0, 0, projs)
                        high(0, 1, projs + 1)
                    if now:
                        rows(PAIRS - 1)
                    if ahead:
                        high(1, 0, projs + 2)
                        for g in range(0, 2 * TB, 2):
                            if g == 2:
                                high(1, 1, projs + 3)
                            act.wait_ge(va_proj, g + 1)
                            if g == 0 and now:
                                act.wait_ge(av_done, 2 * PAIRS)
                            nc.scalar.activation(v_a[:, g // 2, 0:S], ps_s[:, g % 4, :], ACT.Copy).then_inc(va_even, 1)

                @block.vector
                def _(dve):
                    steps = [0]

                    def link(ins):
                        steps[0] += 1
                        ins.then_inc(dve_step, 1)
                        dve.wait_ge(dve_step, steps[0])

                    def statistics():
                        for t in range(TB):
                            ins = nc.vector.bn_stats(stats[:, t, :], x_next[:, t, :])
                        link(ins)
                        for t in range(TB):
                            ins = nc.vector.bn_aggr(mean_var[:, t, :], stats[:, t, :])
                        link(ins)
                        nc.vector.tensor_scalar(rstd[:, :], mean_var[:, :, 1], EPS, None, ALU.add).then_inc(var_ready, 1)

                    def normalise():
                        dve.wait_ge(rstd_ready, 1)
                        for t in range(TB):
                            nc.vector.tensor_scalar(xn_a[:, t, :], x_next[:, t, :], mean_var[:, t, 0:1], rstd[:, t:t + 1],
                                                    ALU.subtract, ALU.mult).then_inc(xn_ready, 1)

                    def x_low(k):
                        dve.wait_ge(xh_ready, k + 1)
                        nc.vector.tensor_tensor(xl_a[:, k, :], ps_m[:, :], xh_a[:, k, :], ALU.subtract).then_inc(xl_ready, 1)

                    def unit_max(u):
                        dve.wait_ge(qk_done, u + 1)
                        nc.vector.reduce_max(neg_max[:, u % 4, :], ps_s[:, 2 * (u % 2):2 * (u % 2) + 2, :], AX.X, negate=True)\
                            .then_inc(max_done, 1)

                    def invert(n):
                        dve.wait_ge(exp_done, 4 * n + 4)
                        nc.vector.reciprocal(recip[:, n % 2, 0:2 * TB], sums[:, n % 2, 0:2 * TB]).then_inc(recip_ready, 1)

                    def low(p, i, m):
                        dve.wait_ge(hi_ready, m + 1)
                        nc.vector.scalar_tensor_tensor(raw_a[:, p % 2, 2 * i + 1, :], ps_m[:, :], SCALE_A if i == 0 else 1.0,
                                                       raw_a[:, p % 2, 2 * i, :], ALU.mult, ALU.subtract).then_inc(lo_ready, 1)

                    def norm(p):
                        dve.wait_ge(rs_ready, p + 1)
                        dve.wait_ge(av_done, 2 * p + 2)
                        nc.vector.tensor_tensor(heads_a[:, p, :], ps_o[:, :], rs_a[:, :], ALU.mult).then_inc(normed, 1)

                    if now:
                        unit_max(0)
                        unit_max(1)
                    if before:
                        for t in range(TB):
                            dve.wait_ge(post_done, t + 1)
                            nc.vector.tensor_tensor(res[:, t, :], res[:, t, :], wide_banks[t][:, 0:D], ALU.add)\
                                .then_inc(x1_ready, 1)
                    if now:
                        for u in range(UNITS):
                            p, r = u // 4, u % 4
                            if r == 0 and p:
                                invert(p - 1)
                            if u + 2 < UNITS:
                                unit_max(u + 2)
                            if u >= 4:
                                dve.wait_ge(av_done, (u - 4) // 2 + 1)
                            dve.wait_ge(tr_done, u + 1)
                            nc.vector.tensor_copy(et_a[:, u % 4, 0:2, :].rearrange("p t s -> p (t s)"), ps_t[:, 0, :])\
                                .then_inc(et_dve, 1)
                            if r == 0 and p:
                                norm(p - 1)
                            if r >= 2 and p + 2 < PAIRS:
                                low(p + 2, r - 2, 2 * p + r - 2)
                            if ahead and u == 21:
                                dve.wait_ge(x_in, 16)
                                statistics()
                            if ahead and u == 24:
                                normalise()
                            if ahead and r == 1 and p >= PAIRS - 2:
                                x_low(p - (PAIRS - 2))
                    if ahead:
                        if not now:
                            statistics()
                            normalise()
                            x_low(0)
                            x_low(1)
                        low(0, 0, projs)
                        low(0, 1, projs + 1)
                    if now:
                        invert(PAIRS - 1)
                        norm(PAIRS - 1)
                    if ahead:
                        low(1, 0, projs + 2)
                        for g in range(1, 2 * TB, 2):
                            if g == 3:
                                low(1, 1, projs + 3)
                            dve.wait_ge(va_proj, g + 1)
                            if g == 1 and now:
                                dve.wait_ge(av_done, 2 * PAIRS)
                            nc.vector.tensor_copy(v_a[:, g // 2, S:DA], ps_s[:, g % 4, :]).then_inc(va_odd, 1)

            next_block()

        attention_a(-1, False, False, True)
        attention_a(0, False, True, True)
        with nc.Fori(1, BATCH - 1) as seq:
            attention_a(seq, True, True, True)
        attention_a(BATCH - 1, True, True, False)
        attention_a(BATCH, True, False, False)

        with nc.Block() as block:
            @block.sync
            def _(sp):
                sp.dma_start(w1_raw[:, :, :], W1T.rearrange("(k p) n -> p k n", p=P)).then_inc(weights_in, 16)
                sp.dma_start(w2_raw[:, :, :], W2T.rearrange("(k p) n -> p k n", p=P)).then_inc(weights_in, 16)
                sp.dma_start(wb_raw[:, :, :], WB.rearrange("(k p) n -> p k n", p=P)).then_inc(weights_in, 16)
                sp.dma_start(cos[:, :], COS).then_inc(weights_in, 16)
                sp.dma_start(sin[:, :], SIN).then_inc(weights_in, 16)
                sp.dma_start(bqk_raw[:, :], BQK).then_inc(weights_in, 16)
                sp.dma_start(b1[:, :], B1).then_inc(weights_in, 16)
                for rows, src in ((bv_rows, BV), (bo_rows, BO), (b2_rows, B2)):
                    sp.dma_start(rows[:, :], src.to_broadcast([P, D])).then_inc(weights_in, 16)
                sp.wait_ge(consts_set, 1)
                for j in range(4):
                    sp.dma_start(wo[32 * j:32 * j + HB, :, :], WO[j]).then_inc(weights_in, 16)
                sp.wait_ge(weights_in, 14 * 16)

            @block.gpsimd
            def _(pool):
                nc.gpsimd.memset(wo[:, :, :], 0.0).then_inc(consts_set, 1)
                nc.gpsimd.memset(ones[:, :], 1.0).then_inc(consts_set, 1)
                nc.gpsimd.memset(k_stack[:, :, :].bitcast(F32), 0.0)
                nc.gpsimd.memset(v_b[:, :, :, :], 0.0)

            @block.tensor
            def _(pe):
                pe.wait_ge(consts_set, 2)
                pe.wait_ge(abs_summed, 2)
                nc.tensor.matmul(ps_m[:, 0:2], ones[:, :], abs_sum[:, :], start=True, stop=True).then_inc(gamma_summed, 1)

            @block.vector
            def _(dve):
                steps = [0]

                def link(ins):
                    steps[0] += 1
                    ins.then_inc(dve_step, 1)
                    dve.wait_ge(dve_step, steps[0])

                dve.wait_ge(weights_in, 14 * 16)
                nc.vector.tensor_reduce(abs_sum[:, 0:1], w1_raw[:, :, :].rearrange("p k n -> p (k n)"), AX.X, ALU.add,
                                        apply_absolute_value=True).then_inc(abs_summed, 1)
                nc.vector.tensor_reduce(abs_sum[:, 1:2], w2_raw[:, :, :].rearrange("p k n -> p (k n)"), AX.X, ALU.add,
                                        apply_absolute_value=True).then_inc(abs_summed, 1)
                link(nc.vector.tensor_copy(wb_hi[:, :, :], wb_raw[:, :, :]))
                nc.vector.tensor_tensor(wb_lo[:, :, :], wb_raw[:, :, :], wb_hi[:, :, :], ALU.subtract)
                nc.vector.tensor_scalar(bqk[:, 0:2], bqk_raw[:, 0:2], SCALE_B, None, ALU.mult)
                nc.vector.tensor_copy(bqk[:, 2:4], bqk_raw[:, 2:4])
                dve.wait_ge(gamma_summed, 1)
                link(nc.vector.tensor_scalar(gamma[:, :], ps_m[:, 0:2], 1.0 / (D * FF), EPS, ALU.mult, ALU.add))
                link(nc.vector.tensor_scalar(half_gamma[:, 0, :], gamma[:, :], 0.5, None, ALU.mult))
                link(nc.vector.tensor_scalar(half_gamma[:, 1, :], gamma[:, :], -0.5, None, ALU.mult))
                for i, (raw, w) in enumerate(((w1_raw, w1), (w2_raw, w2))):
                    flat = raw[:, :, :].rearrange("p k n -> p (k n)")
                    link(nc.vector.tensor_scalar(below[:, :], flat, half_gamma[:, 1, i:i + 1], None, ALU.is_lt))
                    link(nc.vector.scalar_tensor_tensor(w[:, :, :].rearrange("p k n -> p (k n)"), flat,
                                                        half_gamma[:, 0, i:i + 1], below[:, :],
                                                        ALU.is_gt, ALU.subtract))

        next_block()

        with nc.Fori(0, BATCH) as b:
            with nc.Block() as block:

                @block.sync
                def _(sp):
                    sp.dma_start(x[:, :, :], X1[b, :, :].rearrange("(t p) d -> p t d", p=P)).then_inc(x_in, 16)
                    sp.wait_ge(roped, 2)
                    for h in range(H):
                        if h >= 8 and h % 4 == 0:
                            sp.wait_ge(qk_done, 8 * (h // 4 - 1))
                        lanes = slice(8 * h, 8 * h + 8)
                        rows = slice(64 * (h % 2), 64 * (h % 2) + 64)
                        sp.dma_start(q_stack[rows, h // 2 % 4, :].bitcast(F32),
                                     roped_qk[lanes, 0, :, :, :, :].rearrange("p a b c s -> p (a b c) s").bitcast(F32))\
                            .then_inc(b_stacked[h // 2], 16)
                        sp.dma_start(k_stack[rows, h % 8, :].bitcast(F32),
                                     roped_qk[lanes, 1, :, :, :, :].rearrange("p a b c s -> p (a b c) s").bitcast(F32))\
                            .then_inc(b_stacked[h // 2], 16)
                    sp.wait_ge(result, TB)
                    sp.dma_start(OUT[b, :, :].rearrange("(t p) d -> p t d", p=P), x[:, :, :]).then_inc(x_out, 16)
                    sp.wait_ge(x_out, 16)

                @block.gpsimd
                def _(pool):
                    def inverse_deviation(n):
                        pool.wait_ge(var_ready, n + 1)
                        nc.gpsimd.tensor_tensor(rstd[:, :], rstd[:, :], minus_half[:, :], ALU.pow).then_inc(rstd_ready, 1)

                    inverse_deviation(0)
                    inverse_deviation(1)
                    inverse_deviation(2)

                @block.tensor
                def _(pe):
                    mm, tr = nc.tensor.matmul, nc.tensor.transpose

                    def transpose_x(n):
                        for k in range(KT):
                            for t in range(TB):
                                if k == 0:
                                    pe.wait_ge(xn_ready, TB * n + t + 1)
                                last = tr(ps_t[:, k, t * P:(t + 1) * P], xn[:, t, k * P:(k + 1) * P], ident[:, :])
                            last.then_inc(xt_ready, 1)
                        pe.wait_ge(xl_ready, KT * (n + 1))

                    def transposes(u):
                        pe.wait_ge(exp_done, u + 1)
                        unit_transposes(e_b[u % 2]).then_inc(tr_done, 1)

                    def ffn(n):
                        transpose_x(2 * n)

                        def up(f):
                            if f >= 4:
                                pe.wait_ge(relu_done, FT * n + f - 3)
                            todo = [(k, xs) for xs in (xh, xl) for k in range(KT)]
                            for i, (k, xs) in enumerate(todo):
                                last = mm(ps_s[:, f % 4, :], w1[:, k, f * P:(f + 1) * P], xs[:, k, :],
                                          start=(i == 0), stop=(i == len(todo) - 1))
                            last.then_inc(h_proj, 1)

                        for f in range(3):
                            up(f)
                        for f in range(FT):
                            if f + 3 < FT:
                                up(f + 3)
                            pe.wait_ge(h_split, FT * n + f + 1)
                            for t in range(TB):
                                for i, part in enumerate((h_hi, h_lo)):
                                    last = mm(wide_banks[t][:, 0:D], part[:, f, t * P:(t + 1) * P], w2[:, f, :],
                                              start=(f == 0 and i == 0), stop=(f == FT - 1 and i == 1))
                                if f == FT - 1:
                                    last.then_inc(y_done, 1)

                    ffn(0)

                    transpose_x(1)
                    for j in range(4):
                        feature_major(ps_s[:, j, :], xh, xl, wb_hi, wb_lo, j * P).then_inc(bqk_proj, 1)
                    for t in range(TB):
                        token_major(wide_banks[t][:, 0:D], xh, xl, wb_hi, wb_lo, t, 2 * D, D).then_inc(vb_proj, 1)

                    def scores_b(u):
                        half, h = (u // 4) % 2, 4 * (u // 8) + u % 4
                        if h % 2 == 0:
                            pe.wait_ge(b_stacked[h // 2], 4 * 16)
                        if u >= 2:
                            pe.wait_ge(exp_done, u - 1)
                        for j in range(2):
                            c = (2 * half + j) * P
                            last = mm(ps_s[:, 2 * (u % 2) + j, :], q_stack[:, h // 2 % 4, c:c + P], k_stack[:, h % 8, :],
                                      start=True, stop=True)
                        last.then_inc(qk_done, 1)

                    def values_b(n):
                        quad, half = n // 2, n % 2
                        pe.wait_ge(et_act, 4 * n + 4)
                        pe.wait_ge(et_dve, 4 * n + 4)
                        if half == 0 and quad >= 1:
                            pe.wait_ge(normed, quad)
                        for t in range(TB):
                            for h in range(4):
                                last = mm(ps_o[32 * h:32 * (h + 1), half * HS:(half + 1) * HS], v_b[:, t, 4 * quad + h, :],
                                          et_b[:, (4 * n + h) % 6, t, :], start=(t == 0), stop=(t == TB - 1))
                        last.then_inc(av_done, 1)

                    def recip_rows(n):
                        pe.wait_ge(recip_ready, n + 1)
                        if n >= 1:
                            pe.wait_ge(rs_ready, n)
                        reciprocal_products(n, 4, 32).then_inc(rows_ready, 1)

                    pe.wait_ge(vb_ready, TB)
                    scores_b(0)
                    scores_b(1)
                    for u in range(UNITS):
                        if u + 2 < UNITS:
                            scores_b(u + 2)
                        if u % 4 == 0 and u:
                            values_b(u // 4 - 1)
                        if u % 8 == 0 and u:
                            recip_rows(u // 8 - 1)
                        if u >= 1:
                            pe.wait_ge(et_act, u)
                            pe.wait_ge(et_dve, u)
                        transposes(u)
                    values_b(2 * QUADS - 1)
                    recip_rows(QUADS - 1)
                    for g in range(QUADS):
                        pe.wait_ge(normed, g + 1)
                        for t in range(TB):
                            last = mm(ps_s[:, t, 0:D], heads_b[:, g, t * P:(t + 1) * P], wo[:, g, :],
                                      start=(g == 0), stop=(g == QUADS - 1))
                            if g == QUADS - 1:
                                last.then_inc(wo_done, 1)

                    ffn(1)

                @block.scalar
                def _(act):
                    def x_high(n):
                        for k in range(KT):
                            act.wait_ge(xt_ready, KT * n + k + 1)
                            nc.scalar.activation(xh[:, k, :], ps_t[:, k, :], ACT.Copy).then_inc(xh_ready, 1)

                    def exps(u, e, n, i):
                        act.wait_ge(max_done, u + 1)
                        if u >= 2:
                            act.wait_ge(tr_done, u - 1)
                        for j in range(2):
                            ins = nc.scalar.activation(e[u % 2][:, j, :], ps_s[:, 2 * (u % 2) + j, :], ACT.Exp,
                                                       bias=neg_max[:, u % 4, j:j + 1],
                                                       accum_out=sums[:, n % 2, i + j:i + j + 1])
                        ins.then_inc(exp_done, 1)

                    def evacuate(u, et):
                        act.wait_ge(tr_done, u + 1)
                        nc.scalar.activation(et[:, 2:4, :].rearrange("p t s -> p (t s)"), ps_t[:, 1, :], ACT.Copy)\
                            .then_inc(et_act, 1)

                    def rows(n):
                        act.wait_ge(rows_ready, n + 1)
                        if n >= 1:
                            act.wait_ge(normed, n)
                        nc.scalar.activation(rs[:, :], ps_m[:, :], ACT.Copy).then_inc(rs_ready, 1)

                    def ffn(n):
                        x_high(2 * n)
                        for f in range(FT):
                            act.wait_ge(h_proj, FT * n + f + 1)
                            if n or f >= 2:
                                act.wait_ge(h_split, FT * n + f - 1)
                            nc.scalar.activation(h32[:, f % 2, :], ps_s[:, f % 4, :], ACT.Relu,
                                                 bias=b1[:, f:f + 1]).then_inc(relu_done, 1)

                    ffn(0)

                    x_high(1)
                    for j in range(4):
                        act.wait_ge(bqk_proj, j + 1)
                        nc.scalar.activation(qk_flat[j // 2][:, j % 2, :], ps_s[:, j, :], ACT.Identity, bias=bqk[:, j:j + 1],
                                             scale=SCALE_B if j < 2 else 1.0).then_inc(bqk_flat_ready, 1)

                    def exps_b(u):
                        exps(u, e_b, u // 8, (u % 4) * TB + (u // 4) % 2 * 2)

                    exps_b(0)
                    for u in range(UNITS):
                        if u + 1 < UNITS:
                            exps_b(u + 1)
                        if u % 8 == 0 and u:
                            rows(u // 8 - 1)
                        if u >= 6:
                            act.wait_ge(av_done, (u - 6) // 4 + 1)
                        evacuate(u, et_b[:, u % 6, :, :])
                    rows(QUADS - 1)

                    ffn(1)

                @block.vector
                def _(dve):
                    steps = [0]

                    def link(ins):
                        steps[0] += 1
                        ins.then_inc(dve_step, 1)
                        dve.wait_ge(dve_step, steps[0])

                    def layernorm(n):
                        for t in range(TB):
                            ins = nc.vector.bn_stats(stats[:, t, :], x[:, t, :])
                        link(ins)
                        for t in range(TB):
                            ins = nc.vector.bn_aggr(mean_var[:, t, :], stats[:, t, :])
                        link(ins)
                        nc.vector.tensor_scalar(rstd[:, :], mean_var[:, :, 1], EPS, None, ALU.add).then_inc(var_ready, 1)
                        dve.wait_ge(rstd_ready, n + 1)
                        for t in range(TB):
                            nc.vector.tensor_scalar(xn[:, t, :], x[:, t, :], mean_var[:, t, 0:1], rstd[:, t:t + 1],
                                                    ALU.subtract, ALU.mult).then_inc(xn_ready, 1)
                        dve.wait_ge(xn_ready, TB * (n + 1))

                    def x_low(n):
                        for k in range(KT):
                            dve.wait_ge(xh_ready, KT * n + k + 1)
                            nc.vector.tensor_tensor(xl[:, k, :], ps_t[:, k, :], xh[:, k, :], ALU.subtract)\
                                .then_inc(xl_ready, 1)

                    def unit_max(u):
                        dve.wait_ge(qk_done, u + 1)
                        nc.vector.reduce_max(neg_max[:, u % 4, :], ps_s[:, 2 * (u % 2):2 * (u % 2) + 2, :], AX.X, negate=True)\
                            .then_inc(max_done, 1)

                    def invert(n, group):
                        nc.vector.reciprocal(recip[:, n % 2, 0:group * TB], sums[:, n % 2, 0:group * TB]).then_inc(recip_ready, 1)

                    dve.wait_ge(x_in, 16)
                    def ffn(n):
                        layernorm(2 * n)
                        link(nc.vector.tensor_tensor(x[:, :, :], x[:, :, :], rows_of(b2_rows), ALU.add))
                        x_low(2 * n)
                        for f in range(FT):
                            dve.wait_ge(relu_done, FT * n + f + 1)
                            link(nc.vector.tensor_copy(h_hi[:, f, :], h32[:, f % 2, :]))
                            nc.vector.tensor_tensor(h_lo[:, f, :], h32[:, f % 2, :], h_hi[:, f, :], ALU.subtract)\
                                .then_inc(h_split, 1)
                        for t in range(TB):
                            dve.wait_ge(y_done, TB * n + t + 1)
                            ins = nc.vector.tensor_tensor(x[:, t, :], x[:, t, :], wide_banks[t][:, 0:D], ALU.add)
                            if n:
                                ins.then_inc(result, 1)
                        if not n:
                            link(ins)

                    ffn(0)

                    layernorm(1)
                    link(nc.vector.tensor_tensor(x[:, :, :], x[:, :, :], rows_of(bo_rows), ALU.add))
                    x_low(1)
                    for i in range(2):
                        dve.wait_ge(bqk_flat_ready, 2 * i + 2)
                        a, c = qk_flat[i][:, 0, :], qk_flat[i][:, 1, :]
                        nc.vector.tensor_tensor(rot[:, 0, :], a, cos[:, :], ALU.mult)
                        nc.vector.tensor_tensor(rot[:, 1, :], c, sin[:, :], ALU.mult)
                        nc.vector.tensor_tensor(rot[:, 2, :], a, sin[:, :], ALU.mult)
                        link(nc.vector.tensor_tensor(rot[:, 3, :], c, cos[:, :], ALU.mult))
                        nc.vector.tensor_tensor(rot[:, 0, :], rot[:, 0, :], rot[:, 1, :], ALU.subtract)
                        link(nc.vector.tensor_tensor(rot[:, 2, :], rot[:, 2, :], rot[:, 3, :], ALU.add))
                        for half in range(2):
                            if i == 0:
                                high, low = roped_qk[:, 0, half, :, 0, :], roped_qk[:, 0, half, :, 1, :]
                            else:
                                high, low = roped_qk[:, 1, half, 0, :, :], roped_qk[:, 1, half, 1, :, :]
                            turned = rot[:, 2 * half:2 * half + 1, :].to_broadcast([P, 2, S])
                            link(nc.vector.tensor_copy(high, turned))
                            ins = nc.vector.tensor_tensor(low, turned, high, ALU.subtract)
                        ins.then_inc(roped, 1)
                        dve.wait_ge(roped, i + 1)
                    for t in range(TB):
                        dve.wait_ge(vb_proj, t + 1)
                        nc.vector.tensor_tensor(v_b[:, t, :, 0:HB],
                                                wide_banks[t][:, 0:D].rearrange("p (h d) -> p h d", d=HB),
                                                bv_rows[:, :].rearrange("p (h d) -> p h d", d=HB), ALU.add)\
                            .then_inc(vb_ready, 1)

                    def norm_b(g):
                        dve.wait_ge(rs_ready, g + 1)
                        dve.wait_ge(av_done, 2 * g + 2)
                        nc.vector.tensor_tensor(heads_b[:, g, :], ps_o[:, :], rs[:, :], ALU.mult).then_inc(normed, 1)

                    unit_max(0)
                    unit_max(1)
                    for u in range(UNITS):
                        if u % 8 == 0 and u:
                            dve.wait_ge(exp_done, u)
                            invert(u // 8 - 1, 4)
                        if u + 2 < UNITS:
                            unit_max(u + 2)
                        if u >= 6:
                            dve.wait_ge(av_done, (u - 6) // 4 + 1)
                        dve.wait_ge(tr_done, u + 1)
                        nc.vector.tensor_copy(et_b[:, u % 6, 0:2, :].rearrange("p t s -> p (t s)"), ps_t[:, 0, :])\
                            .then_inc(et_dve, 1)
                        if u % 8 == 0 and u:
                            norm_b(u // 8 - 1)
                    dve.wait_ge(exp_done, UNITS)
                    invert(QUADS - 1, 4)
                    norm_b(QUADS - 1)
                    for t in range(TB):
                        dve.wait_ge(wo_done, t + 1)
                        ins = nc.vector.tensor_tensor(x[:, t, :], x[:, t, :], ps_s[:, t, 0:D], ALU.add)
                    link(ins)

                    ffn(1)

            next_block()


def kernel(**inputs):
    import numpy as np
    import concourse.bacc as bacc
    from concourse.bass_utils import run_bass_kernel_spmd

    def get(name):
        return np.asarray(inputs["L0_" + name])

    half, tokens = 8, 512
    pos = np.arange(tokens, dtype=np.float32)[:, None]
    freq = np.float32(1.0) / np.float32(10000.0) ** (np.arange(half, dtype=np.float32) / np.float32(half))
    angles = (pos * freq[None, :]).astype(np.float32)
    cos = np.ascontiguousarray(np.tile(np.cos(angles).astype(np.float32).T, (16, 1)))
    sin = np.ascontiguousarray(np.tile(np.sin(angles).astype(np.float32).T, (16, 1)))

    def halves(w):
        lead = w.shape[:-1]
        return np.swapaxes(w.reshape(*lead, 16, 2, 8), -3, -2).reshape(*lead, 256)

    wb = np.concatenate([halves(get("attn_b_wq_w")), halves(get("attn_b_wk_w")), get("attn_b_wv_w")], axis=1)
    bqk = np.concatenate([halves(get("attn_b_wq_b")), halves(get("attn_b_wk_b"))]).reshape(4, 128).T
    wo = get("attn_b_wo_w").reshape(4, 4, 16, 256).transpose(1, 2, 0, 3)
    arrays = {
        "X": get("attn_a_X"), "WQ": get("attn_a_Wq"), "WK": get("attn_a_Wk"), "WV": get("attn_a_Wv"),
        "WPOST": get("attn_a_Wpost"), "WB": wb, "BQK": bqk, "BV": get("attn_b_wv_b").reshape(1, 256), "WO": wo,
        "BO": get("attn_b_wo_b").reshape(1, 256), "W1T": get("ffn_W1").T, "B1": get("ffn_b1").reshape(8, 128).T,
        "W2T": get("ffn_W2").T, "B2": get("ffn_b2").reshape(1, 256), "COS": cos, "SIN": sin,
    }
    arrays = {name: np.ascontiguousarray(a) for name, a in arrays.items()}
    nc = bacc.Bacc("TRN2", target_bir_lowering=False, num_devices=1)
    args = [nc.dram_tensor(name, a.shape, mybir.dt.from_np(a.dtype), kind="ExternalInput").ap()
            for name, a in arrays.items()]
    x1 = nc.dram_tensor("X1", arrays["X"].shape, mybir.dt.float32, kind="Internal").ap()
    out = nc.dram_tensor("OUT", arrays["X"].shape, mybir.dt.float32, kind="ExternalOutput").ap()
    hybrid_block_kernel(nc, *args, x1, out)
    r = run_bass_kernel_spmd(nc, [arrays], core_ids=[0])
    return r.results[0]["OUT"]
```

```python
import concourse.bass as bass
from concourse import mybir
from contextlib import ExitStack



def hybrid_block_kernel(nc, X, WQ, WK, WV, WPOST, WB, BQK, BV, WO, BO, W1T, B1, W2T, B2, COS, SIN, X1, OUT):
    F32, F32R = mybir.dt.float32, mybir.dt.float32r
    ALU = mybir.AluOpType
    ACT = mybir.ActivationFunctionType
    AX = mybir.AxisListType

    P = 128
    BATCH, S, D = X.shape
    TB = S // P
    KT = D // P
    DA = WQ.shape[1]
    H = 16
    HA = DA // H
    HB = D // H
    PAIRS = H // 2
    FF = W1T.shape[1]
    FT = FF // P
    QUADS = H // 4
    EPS = 1e-5
    SCALE_A = float(HA) ** -0.5
    SCALE_B = float(HB) ** -0.5
    UNITS = 2 * H
    HS = S // 2
    KB = 1024

    ctx = ExitStack()
    with ctx:
        arena = ctx.enter_context(nc.sbuf_tensor("arena", [P, 206 * KB // 4], F32))
        ARENA = nc.lookup_mloc(arena).addr
        arena_end = [0]

        def at(name, kb, shape, dt=F32):
            size = 4
            for n in shape[1:]:
                size *= n
            arena_end[0] = max(arena_end[0], kb * KB + size)
            assert arena_end[0] <= 206 * KB
            return nc.alloc_sbuf_tensor_at(name, shape, dt, offset=ARENA + int(kb * KB))

        ident = at("ident", 0, [P, P])
        rstd = at("rstd", 0.5, [P, TB])
        minus_half = at("minus_half", 0.53125, [P, TB])
        stats = at("stats", 0.5625, [P, TB, 6])
        mean_var = at("mean_var", 0.6875, [P, TB, 2])
        neg_max = at("neg_max", 0.75, [P, 4, 2])
        sums = at("sums", 0.8125, [P, 2, 4 * TB])
        recip = at("recip", 1, [P, 2, 4 * TB])
        abs_sum = at("abs_sum", 1.25, [P, 2])
        gamma = at("gamma", 1.28125, [P, 2])
        half_gamma = at("half_gamma", 1.3125, [P, 2, 2])

        wa_hi = at("wa_hi", 2, [P, KT, 3 * DA], F32R)
        wa_lo = at("wa_lo", 26, [P, KT, 3 * DA], F32R)
        wpost_hi = at("wpost_hi", 50, [P, DA // P, D], F32R)
        wpost_lo = at("wpost_lo", 178, [P, DA // P, D], F32R)
        heads_parts = at("heads_parts", 186, [P, 4, 2, S], F32R)
        xh_a = at("xh_a", 58, [P, KT, S], F32R)
        xl_a = at("xl_a", 62, [P, KT, S], F32R)
        xn_a = at("xn_a", 66, [P, TB, D])
        x_next = at("x_next", 70, [P, TB, D])
        res = at("res", 74, [P, TB, D])
        v_a = at("v_a", 78, [P, TB, DA])
        heads_a = at("heads_a", 94, [P, PAIRS, S])
        stack_a = at("stack_a", 110, [P, 2, 2, 3, S], F32R)
        et_a = at("et_a", 134, [P, 4, TB, HS])
        e_a = (at("e_a0", 150, [P, 2, S]), at("e_a1", 154, [P, 2, S]))
        raw_a = at("raw_a", 158, [P, 2, 4, S], F32R)
        rs_a = at("rs_a", 174, [P, S])
        recip_a = at("recip_a", 176, [P, TB, 2, HA])
        wa_raw = at("wa_raw", 78, [P, KT, 3 * DA])
        wpost_raw = at("wpost_raw", 102, [P, DA // P, D])

        w1 = at("w1", 2, [P, KT, FF], F32R)
        w2 = at("w2", 10, [P, FT, D], F32R)
        wb_hi = at("wb_hi", 18, [P, KT, 3 * D], F32R)
        wb_lo = at("wb_lo", 24, [P, KT, 3 * D], F32R)
        wo = at("wo", 30, [P, QUADS, D])
        cos = at("cos", 34, [P, S])
        sin = at("sin", 36, [P, S])
        bqk = at("bqk", 38, [P, 4])
        bqk_raw = at("bqk_raw", 38.0625, [P, 4])
        b1 = at("b1", 38.125, [P, FT])
        bv_rows = at("bv_rows", 39, [P, D])
        bo_rows = at("bo_rows", 40, [P, D])
        b2_rows = at("b2_rows", 41, [P, D])
        x_ahead = at("x_ahead", 42, [P, TB, D])
        x_before = at("x_before", 46, [P, TB, D])
        xn = at("xn", 50, [P, TB, D])
        xh = at("xh", 54, [P, KT, S], F32R)
        xl = at("xl", 58, [P, KT, S], F32R)
        v_b = at("v_b", 62, [P, TB, H, 32])
        v_next = at("v_next", 70, [P, TB, D])
        k_stack = at("k_stack", 74, [P, H // 2, S], F32R)
        q_stack = at("q_stack", 90, [P, PAIRS // 2, S], F32R)
        et_b = at("et_b", 98, [P, 5, TB, HS])
        e_b = (at("e_b0", 118, [P, 2, S]), at("e_b1", 122, [P, 2, S]))
        roped_qk = at("roped_qk", 126, [P, 2, 2, 2, 2, S], F32R)
        rs = at("rs", 158, [P, S])
        heads_b = at("heads_b", 160, [P, QUADS, S])
        h32 = at("h32", 168, [P, 2, S])
        h_hi = at("h_hi", 172, [P, FT, S], F32R)
        h_lo = at("h_lo", 188, [P, FT, S], F32R)
        qk_flat = (at("q_flat", 172, [P, 2, S]), at("k_flat", 176, [P, 2, S]))
        rot = (at("q_rot", 180, [P, 4, S]), at("k_rot", 196, [P, 4, S]))
        recip_b = at("recip_b", 204, [P, 2, 4, 32])
        w1_raw = at("w1_raw", 114, [P, KT, FF])
        w2_raw = at("w2_raw", 122, [P, FT, D])
        wb_raw = at("wb_raw", 130, [P, KT, 3 * D])
        below = at("below", 136, [P, KT * FF])
        ones = at("ones", 144, [P, P])

        def ps(name, shape):
            return ctx.enter_context(nc.psum_tensor(name, shape, F32))

        ps_s = ps("ps_s", [P, 4, S])
        ps_t = ps("ps_t", [P, 2, S])
        ps_o = ps("ps_o", [P, S])
        ps_m = ps("ps_m", [P, S])
        wide_banks = [ps_t[:, 0, :], ps_t[:, 1, :], ps_o[:, :], ps_m[:, :]]

        ids = []

        def sem(name):
            h = ctx.enter_context(nc.semaphore(name))
            ids.append(h.num)
            return h

        weights_in = sem("weights_in")
        matrix_in = [sem(f"matrix_in{i}") for i in range(4)]
        consts_set = sem("consts_set")
        abs_summed = sem("abs_summed")
        gamma_summed = sem("gamma_summed")
        dve_step = sem("dve_step")
        x_in = sem("x_in")
        x_out = sem("x_out")
        var_ready = sem("var_ready")
        rstd_ready = sem("rstd_ready")
        xn_ready = sem("xn_ready")
        xt_ready = sem("xt_ready")
        xh_ready = sem("xh_ready")
        xl_ready = sem("xl_ready")
        va_proj = sem("va_proj")
        va_even = sem("va_even")
        va_odd = sem("va_odd")
        proj_ready = sem("proj_ready")
        hi_ready = sem("hi_ready")
        lo_ready = sem("lo_ready")
        qk_done = sem("qk_done")
        max_done = sem("max_done")
        exp_done = sem("exp_done")
        tr_done = sem("tr_done")
        et_act = sem("et_act")
        et_dve = sem("et_dve")
        av_done = sem("av_done")
        recip_ready = sem("recip_ready")
        rows_ready = sem("rows_ready")
        rs_ready = sem("rs_ready")
        normed = sem("normed")
        gelu_done = sem("gelu_done")
        heads_split = sem("heads_split")
        parts_used = sem("parts_used")
        post_done = sem("post_done")
        x1_ready = sem("x1_ready")
        res_ready = sem("res_ready")
        h_split = sem("h_split")
        bank_filled = sem("bank_filled")
        bank_freed = [sem(f"bank_freed{i}") for i in range(4)]
        hi_copied = sem("hi_copied")
        biased = sem("biased")
        stats_ready = sem("stats_ready")
        rope_step = sem("rope_step")
        turned = sem("turned")
        high_ready = sem("high_ready")
        before_in = sem("before_in")
        roped = sem("roped")
        stacked = [sem("stacked0"), sem("stacked1")]
        b_stacked = [sem(f"b_stacked{i}") for i in range(PAIRS)]
        every_sem = range(min(ids), max(ids) + 1)

        def next_block():
            nc.all_engine_barrier(sems_to_clear=every_sem)

        def rows_of(tile):
            return tile[:, :].rearrange("p (o d) -> p o d", o=1).to_broadcast([P, TB, D])

        def passes(xs_hi, xs_lo, hi, lo):
            for k in range(KT):
                yield k, xs_hi, hi
                yield k, xs_hi, lo
            for k in range(KT):
                yield k, xs_lo, hi

        def feature_major(out, xs_hi, xs_lo, hi, lo, c0):
            todo = list(passes(xs_hi, xs_lo, hi, lo))
            for i, (k, xs, w) in enumerate(todo):
                last = nc.tensor.matmul(out, w[:, k, c0:c0 + P], xs[:, k, :], start=(i == 0), stop=(i == len(todo) - 1))
            return last

        def token_major(out, xs_hi, xs_lo, hi, lo, t, c0, n):
            todo = list(passes(xs_hi, xs_lo, hi, lo))
            for i, (k, xs, w) in enumerate(todo):
                last = nc.tensor.matmul(out, xs[:, k, t * P:(t + 1) * P], w[:, k, c0:c0 + n],
                                        start=(i == 0), stop=(i == len(todo) - 1))
            return last

        def unit_transposes(e):
            for t in range(TB):
                for j in range(2):
                    c = (t % 2) * HS + j * P
                    last = nc.tensor.transpose(ps_t[:, t // 2, c:c + P], e[:, j, t * P:(t + 1) * P], ident[:, :])
            return last

        def reciprocal_products(wide):
            for t in range(TB):
                last = nc.tensor.transpose(ps_m[:, t * P:(t + 1) * P], wide[:, t, :, :].rearrange("p h w -> p (h w)"),
                                           ident[:, :])
            return last

        with nc.Block() as block:

            @block.sync
            def _(sp):
                for i, w in enumerate((WQ, WK, WV)):
                    sp.dma_start(wa_raw[:, :, i * DA:(i + 1) * DA],
                                 w.rearrange("(k p) n -> p k n", p=P)).then_inc(matrix_in[i], 16)
                sp.dma_start(wpost_raw[:, :, :], WPOST.rearrange("(k p) n -> p k n", p=P)).then_inc(matrix_in[3], 16)
                sp.dma_start(x_next[:, :, :], X[0, :, :].rearrange("(t p) d -> p t d", p=P)).then_inc(weights_in, 16)
                sp.wait_ge(weights_in, 16)

            @block.gpsimd
            def _(pool):
                nc.gpsimd.memset(minus_half[:, :], -0.5)
                nc.gpsimd.memset(ident[:, :], 0.0).then_inc(consts_set, 1)
                pool.wait_ge(consts_set, 1)
                nc.gpsimd.affine_select(out=ident[:, :], in_=ident[:, :], compare_op=ALU.not_equal, fill=1.0,
                                        base=0, pattern=[[-1, P]], channel_multiplier=1).then_inc(consts_set, 1)

            @block.vector
            def _(dve):
                for i in range(4):
                    columns = slice(i * DA, (i + 1) * DA)
                    raw, high, low = ((wa_raw[:, :, columns], wa_hi[:, :, columns], wa_lo[:, :, columns]) if i < 3 else
                                      (wpost_raw[:, :, :], wpost_hi[:, :, :], wpost_lo[:, :, :]))
                    dve.wait_ge(matrix_in[i], 16)
                    nc.vector.tensor_copy(high, raw).then_inc(dve_step, 1)
                    dve.wait_ge(dve_step, i + 1)
                    nc.vector.tensor_tensor(low, raw, high, ALU.subtract)

        next_block()

        def attention_a(seq, before, now, ahead):
            projs = 2 * (PAIRS - 2) if now else 0
            pair_stacks = 6 * 16
            place = (PAIRS - 2) // 2 * pair_stacks if now else 0

            with nc.Block() as block:

                @block.sync
                def _(sp):
                    def stack(p, at_proj):
                        sp.wait_ge(lo_ready, at_proj + 2)
                        raw = raw_a[:, p % 2, :, :].bitcast(F32)
                        for h in range(2):
                            src = slice(HA * h, HA * (h + 1))
                            dst = stack_a[:, p % 2, h, :, :].bitcast(F32)
                            sp.dma_start(dst[0:HA, 0, :], raw[src, 0, :]).then_inc(stacked[p % 2], 16)
                            sp.dma_start(dst[0:HA, 1:3, :], raw[src, 2:4, :]).then_inc(stacked[p % 2], 16)
                            sp.dma_start(dst[HA:P, :, :], raw[src, 1:4, :]).then_inc(stacked[p % 2], 16)

                    if before:
                        sp.wait_ge(x1_ready, TB)
                        sp.dma_start(X1[seq - 1, :, :].rearrange("(t p) d -> p t d", p=P), res[:, :, :]).then_inc(x_out, 16)
                    if now:
                        for p in range(2, PAIRS):
                            sp.wait_ge(qk_done, 4 * (p - 1))
                            stack(p, 2 * (p - 2))
                            if p == 3 and ahead:
                                sp.wait_ge(res_ready, 1)
                                sp.dma_start(x_next[:, :, :], X[seq + 1, :, :].rearrange("(t p) d -> p t d", p=P))\
                                    .then_inc(x_in, 16)
                    if ahead:
                        for p in range(2):
                            if now:
                                sp.wait_ge(qk_done, 4 * (PAIRS - 1 + p))
                            stack(p, projs + 2 * p)
                        for p in range(2):
                            sp.wait_ge(stacked[p], place + pair_stacks)
                    if before:
                        sp.wait_ge(x_out, 16)

                @block.gpsimd
                def _(pool):
                    def inverse_deviation():
                        pool.wait_ge(var_ready, 1)
                        nc.gpsimd.tensor_tensor(rstd[:, :], rstd[:, :], minus_half[:, :], ALU.pow).then_inc(rstd_ready, 1)

                    if now:
                        if before:
                            pool.wait_ge(x_out, 16)
                        nc.gpsimd.tensor_tensor(res[:, :, :], x_next[:, :, :], xn_a[:, :, :], ALU.add).then_inc(res_ready, 1)
                    if ahead:
                        inverse_deviation()

                @block.tensor
                def _(pe):
                    mm = nc.tensor.matmul

                    def scores(u):
                        p, half, h = u // 4, (u // 2) % 2, u % 2
                        if u % 4 == 0 and p >= 2:
                            pe.wait_ge(stacked[p % 2], (p // 2) * pair_stacks)
                        if u >= 2:
                            pe.wait_ge(exp_done, u - 1)
                        st = stack_a[:, p % 2, h, :, :]
                        for j in range(2):
                            c = (2 * half + j) * P
                            out = ps_s[:, 2 * (u % 2) + j, :]
                            mm(out, st[:, 0, c:c + P], st[:, 1, :], start=True, stop=False)
                            last = mm(out, st[:, 0, c:c + P], st[:, 2, :], start=False, stop=True)
                        last.then_inc(qk_done, 1)

                    def values(n):
                        p, half = n // 2, n % 2
                        pe.wait_ge(et_act, 2 * n + 2)
                        pe.wait_ge(et_dve, 2 * n + 2)
                        if half == 0 and p >= 1:
                            pe.wait_ge(normed, p)
                        if n == 0 and before:
                            pe.wait_ge(x1_ready, TB)
                        for t in range(TB):
                            for h in range(2):
                                c = (2 * p + h) * HA
                                last = mm(ps_o[HA * h:HA * (h + 1), half * HS:(half + 1) * HS], v_a[:, t, c:c + HA],
                                          et_a[:, (2 * n + h) % 4, t, :], start=(t == 0), stop=(t == TB - 1))
                        last.then_inc(av_done, 1)

                    def recip_rows(n):
                        pe.wait_ge(recip_ready, n + 1)
                        reciprocal_products(recip_a).then_inc(rows_ready, 1)

                    def project(p, i):
                        feature_major(ps_m[:, :], xh_a, xl_a, wa_hi, wa_lo, i * DA + p * P).then_inc(proj_ready, 1)

                    def project_ahead(m):
                        if m == 0:
                            pe.wait_ge(xl_ready, KT)
                        else:
                            pe.wait_ge(lo_ready, projs + m)
                        project(m // 2, m % 2)

                    def transpose_x(k):
                        if k == 0:
                            pe.wait_ge(xn_ready, TB)
                        else:
                            pe.wait_ge(xl_ready, k)
                        for t in range(TB):
                            last = nc.tensor.transpose(ps_m[:, t * P:(t + 1) * P], xn_a[:, t, k * P:(k + 1) * P], ident[:, :])
                        last.then_inc(xt_ready, 1)

                    if now:
                        scores(0)
                        scores(1)
                    if before:
                        for k in range(PAIRS):
                            if k >= 4:
                                pe.wait_ge(heads_split, k - 3)
                            for t in range(TB):
                                for i, (part, w) in enumerate(((0, wpost_hi), (0, wpost_lo), (1, wpost_hi))):
                                    last = mm(wide_banks[t][:, 0:D], heads_parts[:, k % 4, part, t * P:(t + 1) * P],
                                              w[:, k, :], start=(k == 0 and i == 0), stop=(k == PAIRS - 1 and i == 2))
                                if k == PAIRS - 1:
                                    last.then_inc(post_done, 1)
                            if k < PAIRS - 1:
                                last.then_inc(parts_used, 1)
                    if now:
                        for u in range(UNITS):
                            p, r = u // 4, u % 4
                            if u + 2 < UNITS:
                                scores(u + 2)
                            if u >= 1:
                                pe.wait_ge(et_act, u)
                                pe.wait_ge(et_dve, u)
                            elif before:
                                pe.wait_ge(x1_ready, TB)
                            pe.wait_ge(exp_done, u + 1)
                            unit_transposes(e_a[u % 2]).then_inc(tr_done, 1)
                            if r == 0 and p:
                                values(2 * p - 1)
                                if p <= PAIRS - 2:
                                    pe.wait_ge(lo_ready, 2 * p)
                                elif ahead:
                                    pe.wait_ge(xl_ready, KT)
                                else:
                                    pe.wait_ge(rs_ready, p - 1)
                                recip_rows(p - 1)
                            if r == 3:
                                values(2 * p)
                            if r in (1, 2) and p + 2 < PAIRS:
                                if r == 1 and p:
                                    pe.wait_ge(rs_ready, p)
                                if r == 2:
                                    pe.wait_ge(lo_ready, 2 * p + 1)
                                project(p + 2, r - 1)
                            if ahead and r in (1, 2) and p == PAIRS - 2:
                                if r == 1:
                                    pe.wait_ge(rs_ready, p)
                                transpose_x(r - 1)
                            if ahead and r >= 1 and p == PAIRS - 1:
                                if r == 1:
                                    pe.wait_ge(rs_ready, p)
                                project_ahead(r - 1)
                    if ahead and not now:
                        for k in range(KT):
                            transpose_x(k)
                        for m in range(3):
                            project_ahead(m)
                    if now:
                        values(2 * PAIRS - 1)
                    if ahead:
                        project_ahead(3)
                    if now and not ahead:
                        pe.wait_ge(rs_ready, PAIRS - 1)
                        recip_rows(PAIRS - 1)
                    if ahead:
                        for g in range(2 * TB):
                            if g >= 4:
                                pe.wait_ge((va_even, va_odd)[g % 2], (g - 4) // 2 + 1)
                            token_major(ps_s[:, g % 4, :], xh_a, xl_a, wa_hi, wa_lo, g // 2, 2 * DA + (g % 2) * S, S)\
                                .then_inc(va_proj, 1)
                            if g == 0 and now:
                                pe.wait_ge(lo_ready, projs + 4)
                                recip_rows(PAIRS - 1)

                @block.scalar
                def _(act):
                    def exps(u):
                        p, half, h = u // 4, (u // 2) % 2, u % 2
                        act.wait_ge(max_done, u + 1)
                        if u >= 2:
                            act.wait_ge(tr_done, u - 1)
                        for j in range(2):
                            c = h * TB + 2 * half + j
                            ins = nc.scalar.activation(e_a[u % 2][:, j, :], ps_s[:, 2 * (u % 2) + j, :], ACT.Exp,
                                                       bias=neg_max[:, u % 4, j:j + 1], accum_out=sums[:, p % 2, c:c + 1])
                        ins.then_inc(exp_done, 1)

                    def high(p, i, m):
                        act.wait_ge(proj_ready, m + 1)
                        if i == 0 and m >= 4:
                            act.wait_ge(stacked[p % 2], ((m - 4) // 4 + 1) * pair_stacks)
                        nc.scalar.activation(raw_a[:, p % 2, 2 * i, :], ps_m[:, :], ACT.Copy,
                                             scale=SCALE_A if i == 0 else 1.0).then_inc(hi_ready, 1)

                    def x_high(k):
                        act.wait_ge(xt_ready, k + 1)
                        nc.scalar.activation(xh_a[:, k, :], ps_m[:, :], ACT.Copy).then_inc(xh_ready, 1)

                    def rows(n):
                        act.wait_ge(rows_ready, n + 1)
                        if n >= 1:
                            act.wait_ge(normed, n)
                        nc.scalar.activation(rs_a[:, :], ps_m[:, :], ACT.Copy).then_inc(rs_ready, 1)

                    def gelu(k):
                        act.wait_ge(normed, k + 1)
                        nc.scalar.activation(heads_a[:, k, :], heads_a[:, k, :], ACT.Gelu).then_inc(gelu_done, 1)

                    if now:
                        exps(0)
                        for u in range(UNITS):
                            p, r = u // 4, u % 4
                            if u + 1 < UNITS:
                                exps(u + 1)
                            if r == 1 and p:
                                rows(p - 1)
                            if u >= 4:
                                act.wait_ge(av_done, (u - 4) // 2 + 1)
                            act.wait_ge(tr_done, u + 1)
                            nc.scalar.activation(et_a[:, u % 4, 2:4, :].rearrange("p t s -> p (t s)"), ps_t[:, 1, :],
                                                 ACT.Copy).then_inc(et_act, 1)
                            if r in (1, 2) and p + 2 < PAIRS:
                                high(p + 2, r - 1, 2 * p + r - 1)
                            if ahead and r in (1, 2) and p == PAIRS - 2:
                                x_high(r - 1)
                            if ahead and r >= 1 and p == PAIRS - 1:
                                high((r - 1) // 2, (r - 1) % 2, projs + r - 1)
                    if ahead and not now:
                        for k in range(KT):
                            x_high(k)
                        for m in range(3):
                            high(m // 2, m % 2, m)
                    if ahead:
                        high(1, 1, projs + 3)
                        for g in range(0, 2 * TB, 2):
                            act.wait_ge(va_proj, g + 1)
                            if g == 0 and now:
                                act.wait_ge(av_done, 2 * PAIRS)
                            nc.scalar.activation(v_a[:, g // 2, 0:S], ps_s[:, g % 4, :], ACT.Copy).then_inc(va_even, 1)
                            if g == 0 and now:
                                rows(PAIRS - 1)
                            if now:
                                gelu(g)
                                gelu(g + 1)
                    elif now:
                        rows(PAIRS - 1)
                        for k in range(PAIRS):
                            gelu(k)

                @block.vector
                def _(dve):
                    steps = [0]

                    def link(ins):
                        steps[0] += 1
                        ins.then_inc(dve_step, 1)
                        dve.wait_ge(dve_step, steps[0])

                    def statistics():
                        for t in range(TB):
                            ins = nc.vector.bn_stats(stats[:, t, :], x_next[:, t, :])
                        link(ins)
                        for t in range(TB):
                            ins = nc.vector.bn_aggr(mean_var[:, t, :], stats[:, t, :])
                        link(ins)
                        nc.vector.tensor_scalar(rstd[:, :], mean_var[:, :, 1], EPS, None, ALU.add).then_inc(var_ready, 1)

                    def normalise():
                        dve.wait_ge(rstd_ready, 1)
                        for t in range(TB):
                            nc.vector.tensor_scalar(xn_a[:, t, :], x_next[:, t, :], mean_var[:, t, 0:1], rstd[:, t:t + 1],
                                                    ALU.subtract, ALU.mult).then_inc(xn_ready, 1)

                    def x_low(k):
                        dve.wait_ge(xh_ready, k + 1)
                        nc.vector.tensor_tensor(xl_a[:, k, :], ps_m[:, :], xh_a[:, k, :], ALU.subtract).then_inc(xl_ready, 1)

                    def unit_max(u):
                        dve.wait_ge(qk_done, u + 1)
                        nc.vector.reduce_max(neg_max[:, u % 4, :], ps_s[:, 2 * (u % 2):2 * (u % 2) + 2, :], AX.X, negate=True)\
                            .then_inc(max_done, 1)

                    def invert(n):
                        dve.wait_ge(exp_done, 4 * n + 4)
                        if n >= 1:
                            dve.wait_ge(rows_ready, n)
                        link(nc.vector.reciprocal(recip[:, n % 2, 0:2 * TB], sums[:, n % 2, 0:2 * TB]))
                        src = recip[:, n % 2, 0:2 * TB].rearrange("p (h t o) -> p t h o", t=TB, o=1)
                        nc.vector.tensor_copy(recip_a[:, :, :, :], src.to_broadcast([P, TB, 2, HA])).then_inc(recip_ready, 1)

                    def low(p, i, m):
                        dve.wait_ge(hi_ready, m + 1)
                        nc.vector.scalar_tensor_tensor(raw_a[:, p % 2, 2 * i + 1, :], ps_m[:, :], SCALE_A if i == 0 else 1.0,
                                                       raw_a[:, p % 2, 2 * i, :], ALU.mult, ALU.subtract).then_inc(lo_ready, 1)

                    def norm(p):
                        dve.wait_ge(rs_ready, p + 1)
                        dve.wait_ge(av_done, 2 * p + 2)
                        nc.vector.tensor_tensor(heads_a[:, p, :], ps_o[:, :], rs_a[:, :], ALU.mult).then_inc(normed, 1)

                    def split_heads(k):
                        if k < 4:
                            dve.wait_ge(gelu_done, k + 1)
                        else:
                            dve.wait_ge(parts_used, k - 3)
                        link(nc.vector.tensor_copy(heads_parts[:, k % 4, 0, :], heads_a[:, k, :]))
                        nc.vector.tensor_tensor(heads_parts[:, k % 4, 1, :], heads_a[:, k, :], heads_parts[:, k % 4, 0, :],
                                                ALU.subtract).then_inc(heads_split, 1)

                    if now:
                        unit_max(0)
                        unit_max(1)
                    if before:
                        for k in range(4, PAIRS):
                            split_heads(k)
                        for t in range(TB):
                            dve.wait_ge(post_done, t + 1)
                            nc.vector.tensor_tensor(res[:, t, :], res[:, t, :], wide_banks[t][:, 0:D], ALU.add)\
                                .then_inc(x1_ready, 1)
                    if now:
                        for u in range(UNITS):
                            p, r = u // 4, u % 4
                            if r == 0 and p:
                                invert(p - 1)
                            if u + 2 < UNITS:
                                unit_max(u + 2)
                            if u >= 4:
                                dve.wait_ge(av_done, (u - 4) // 2 + 1)
                            dve.wait_ge(tr_done, u + 1)
                            nc.vector.tensor_copy(et_a[:, u % 4, 0:2, :].rearrange("p t s -> p (t s)"), ps_t[:, 0, :])\
                                .then_inc(et_dve, 1)
                            if r == 1 and p:
                                norm(p - 1)
                            if r in (1, 2) and p + 2 < PAIRS:
                                low(p + 2, r - 1, 2 * p + r - 1)
                            if ahead and u == 20:
                                dve.wait_ge(x_in, 16)
                                statistics()
                            if ahead and u == 23:
                                normalise()
                            if ahead and r in (1, 2) and p == PAIRS - 2:
                                x_low(r - 1)
                            if ahead and r >= 1 and p == PAIRS - 1:
                                low((r - 1) // 2, (r - 1) % 2, projs + r - 1)
                    if now:
                        invert(PAIRS - 1)
                    if ahead and not now:
                        statistics()
                        normalise()
                        for k in range(KT):
                            x_low(k)
                        for m in range(3):
                            low(m // 2, m % 2, m)
                    if ahead:
                        low(1, 1, projs + 3)
                        for g in range(1, 2 * TB, 2):
                            dve.wait_ge(va_proj, g + 1)
                            if g == 1 and now:
                                dve.wait_ge(av_done, 2 * PAIRS)
                            nc.vector.tensor_copy(v_a[:, g // 2, S:DA], ps_s[:, g % 4, :]).then_inc(va_odd, 1)
                            if g == 1 and now:
                                norm(PAIRS - 1)
                            if now:
                                for k in ((0,), (1, 2), (3,), ())[g // 2]:
                                    split_heads(k)
                    elif now:
                        norm(PAIRS - 1)
                        for k in range(4):
                            split_heads(k)
                    if now:
                        dve.wait_ge(gelu_done, PAIRS)

            next_block()

        attention_a(-1, False, False, True)
        attention_a(0, False, True, True)
        with nc.Fori(1, BATCH - 1) as seq:
            attention_a(seq, True, True, True)
        attention_a(BATCH - 1, True, True, False)
        attention_a(BATCH, True, False, False)

        with nc.Block() as block:
            @block.sync
            def _(sp):
                sp.dma_start(w1_raw[:, :, :], W1T.rearrange("(k p) n -> p k n", p=P)).then_inc(matrix_in[0], 16)
                sp.dma_start(w2_raw[:, :, :], W2T.rearrange("(k p) n -> p k n", p=P)).then_inc(matrix_in[1], 16)
                sp.dma_start(wb_raw[:, :, :], WB.rearrange("(k p) n -> p k n", p=P)).then_inc(matrix_in[2], 16)
                sp.dma_start(cos[:, :], COS).then_inc(weights_in, 16)
                sp.dma_start(sin[:, :], SIN).then_inc(weights_in, 16)
                sp.dma_start(bqk_raw[:, :], BQK).then_inc(weights_in, 16)
                sp.dma_start(b1[:, :], B1).then_inc(weights_in, 16)
                for rows, src in ((bv_rows, BV), (bo_rows, BO), (b2_rows, B2)):
                    sp.dma_start(rows[:, :], src.to_broadcast([P, D])).then_inc(weights_in, 16)
                sp.wait_ge(consts_set, 1)
                for j in range(4):
                    sp.dma_start(wo[32 * j:32 * j + HB, :, :], WO[j]).then_inc(weights_in, 16)
                sp.wait_ge(weights_in, 11 * 16)

            @block.gpsimd
            def _(pool):
                nc.gpsimd.memset(wo[:, :, :], 0.0).then_inc(consts_set, 1)
                nc.gpsimd.memset(ones[:, :], 1.0).then_inc(consts_set, 1)
                nc.gpsimd.memset(k_stack[:, :, :].bitcast(F32), 0.0)
                nc.gpsimd.memset(v_b[:, :, :, :], 0.0)

            @block.tensor
            def _(pe):
                pe.wait_ge(consts_set, 2)
                pe.wait_ge(abs_summed, 2)
                nc.tensor.matmul(ps_m[:, 0:2], ones[:, :], abs_sum[:, :], start=True, stop=True).then_inc(gamma_summed, 1)

            @block.vector
            def _(dve):
                steps = [0]

                def link(ins):
                    steps[0] += 1
                    ins.then_inc(dve_step, 1)
                    dve.wait_ge(dve_step, steps[0])

                dve.wait_ge(matrix_in[0], 16)
                nc.vector.tensor_reduce(abs_sum[:, 0:1], w1_raw[:, :, :].rearrange("p k n -> p (k n)"), AX.X, ALU.add,
                                        apply_absolute_value=True).then_inc(abs_summed, 1)
                dve.wait_ge(matrix_in[1], 16)
                nc.vector.tensor_reduce(abs_sum[:, 1:2], w2_raw[:, :, :].rearrange("p k n -> p (k n)"), AX.X, ALU.add,
                                        apply_absolute_value=True).then_inc(abs_summed, 1)
                dve.wait_ge(matrix_in[2], 16)
                link(nc.vector.tensor_copy(wb_hi[:, :, :], wb_raw[:, :, :]))
                nc.vector.tensor_tensor(wb_lo[:, :, :], wb_raw[:, :, :], wb_hi[:, :, :], ALU.subtract)
                dve.wait_ge(weights_in, 11 * 16)
                nc.vector.tensor_scalar(bqk[:, 0:2], bqk_raw[:, 0:2], SCALE_B, None, ALU.mult)
                nc.vector.tensor_copy(bqk[:, 2:4], bqk_raw[:, 2:4])
                dve.wait_ge(gamma_summed, 1)
                link(nc.vector.tensor_scalar(gamma[:, :], ps_m[:, 0:2], 1.0 / (D * FF), EPS, ALU.mult, ALU.add))
                link(nc.vector.tensor_scalar(half_gamma[:, 0, :], gamma[:, :], 0.5, None, ALU.mult))
                link(nc.vector.tensor_scalar(half_gamma[:, 1, :], gamma[:, :], -0.5, None, ALU.mult))
                for i, (raw, w) in enumerate(((w1_raw, w1), (w2_raw, w2))):
                    flat = raw[:, :, :].rearrange("p k n -> p (k n)")
                    link(nc.vector.tensor_scalar(below[:, :], flat, half_gamma[:, 1, i:i + 1], None, ALU.is_lt))
                    link(nc.vector.scalar_tensor_tensor(w[:, :, :].rearrange("p k n -> p (k n)"), flat,
                                                        half_gamma[:, 0, i:i + 1], below[:, :],
                                                        ALU.is_gt, ALU.subtract))

        next_block()

        def free_at(h, quad):
            return 8 * quad + 4 + (h % 4 | 1) + 1

        def attention_b(seq, before, now, ahead):
            norms = (["ffn0", "attn"] if ahead else []) + (["ffn1"] if before else [])
            ffns = (["ffn0"] if ahead else []) + (["ffn1"] if before else [])
            plan = []
            if before:
                plan += [(t - 2, "wo", "ffn1", t) for t in range(TB)]
                plan += [(XT1 + k, "transpose", "ffn1", k) for k in range(KT)]
                plan += [(UP1[f], "up", "ffn1", f) for f in range(FT)]
                plan += [(DOWN1[t], "down", "ffn1", t) for t in range(TB)]
            if now:
                plan += [(8 * n + 8.5, "recip", "attn", n) for n in range(2 * QUADS)]
                plan += [(8 * n + 9.5, "values", "attn", n) for n in range(2 * QUADS)]
            if ahead:
                plan += [(XT0 + k, "transpose", "ffn0", k) for k in range(KT)]
                plan += [(UP0[f], "up", "ffn0", f) for f in range(FT)]
                plan += [(DOWN0[t], "down", "ffn0", t) for t in range(TB)]
                plan += [(XTB + k, "transpose", "attn", k) for k in range(KT)]
                plan += [(QK[j], "qk", "attn", j) for j in range(4)]
                plan += [(VB[t], "v", "attn", t) for t in range(TB)]
            step, fills = {}, 0
            for s, kind, part, i in sorted(plan):
                if kind in ("wo", "down", "v"):
                    step[s] = (kind, part, i, fills)
                    fills += i % 2
                else:
                    step[s] = (kind, part, i, fills)
                    fills += 1
            banks = [ps_m[:, :], ps_o[:, :]] if now else [ps_s[:, i, :] for i in range(4)]

            def bank(fill):
                return banks[fill % len(banks)]

            def wait_emptied(engine, fill):
                engine.wait_ge(bank_freed[fill % len(banks)], fill // len(banks) + 1)

            def emptied(ins, fill):
                ins.then_inc(bank_freed[fill % len(banks)], 1)

            fill_of = {(kind, part, i): fill for kind, part, i, fill in step.values()}
            x_of = {"ffn0": x_ahead, "attn": x_ahead, "ffn1": x_before}

            with nc.Block() as block:

                @block.sync
                def _(sp):
                    if ahead:
                        sp.dma_start(x_ahead[:, :, :], X1[seq + 1, :, :].rearrange("(t p) d -> p t d", p=P)).then_inc(x_in, 16)
                    if before:
                        sp.dma_start(x_before[:, :, :], X1[seq - 1, :, :].rearrange("(t p) d -> p t d", p=P))\
                            .then_inc(before_in, 16)

                    def stack(h):
                        lanes = slice(8 * h, 8 * h + 8)
                        rows = slice(64 * (h % 2), 64 * (h % 2) + 64)
                        sp.dma_start(q_stack[rows, h // 2 % 4, :].bitcast(F32),
                                     roped_qk[lanes, 0, :, :, :, :].rearrange("p a b c s -> p (a b c) s").bitcast(F32))\
                            .then_inc(b_stacked[h // 2], 16)
                        sp.dma_start(k_stack[rows, h % 8, :].bitcast(F32),
                                     roped_qk[lanes, 1, :, :, :, :].rearrange("p a b c s -> p (a b c) s").bitcast(F32))\
                            .then_inc(b_stacked[h // 2], 16)

                    if now:
                        for h in range(8, H):
                            sp.wait_ge(qk_done, free_at(h, h // 4 - 2))
                            stack(h)
                    if ahead:
                        sp.wait_ge(biased, norms.index("attn") + 1)
                        sp.dma_start(X1[seq + 1, :, :].rearrange("(t p) d -> p t d", p=P), x_ahead[:, :, :]).then_inc(x_out, 16)
                        sp.wait_ge(roped, 4)
                        for h in range(4):
                            if now:
                                sp.wait_ge(qk_done, free_at(h, 2))
                            stack(h)
                    if before:
                        wait_emptied(sp, fill_of["down", "ffn1", 1])
                        wait_emptied(sp, fill_of["down", "ffn1", TB - 1])
                        sp.dma_start(OUT[seq - 1, :, :].rearrange("(t p) d -> p t d", p=P), x_before[:, :, :])\
                            .then_inc(x_out, 16)
                    if ahead:
                        for h in range(4, 8):
                            if now:
                                sp.wait_ge(qk_done, free_at(h, 3))
                            stack(h)
                        for pair in range(4):
                            sp.wait_ge(b_stacked[pair], 4 * 16)
                    sp.wait_ge(x_out, 16 * (before + ahead))

                @block.gpsimd
                def _(pool):
                    def inverse_deviation(part):
                        n = norms.index(part)
                        pool.wait_ge(var_ready, n + 1)
                        nc.gpsimd.tensor_tensor(rstd[:, :], rstd[:, :], minus_half[:, :], ALU.pow).then_inc(rstd_ready, 1)

                    def add_bias(part):
                        pool.wait_ge(xn_ready, TB * (norms.index(part) + 1))
                        nc.gpsimd.tensor_tensor(x_of[part][:, :, :], x_of[part][:, :, :],
                                                rows_of(bo_rows if part == "attn" else b2_rows), ALU.add).then_inc(biased, 1)

                    def hidden_low(s):
                        if s in step and step[s][0] == "up":
                            kind, part, i, fill = step[s]
                            pool.wait_ge(hi_copied, FT * ffns.index(part) + i + 1)
                            nc.gpsimd.tensor_tensor(h_lo[:, i, :], h32[:, i % 2, :], h_hi[:, i, :], ALU.subtract)\
                                .then_inc(h_split, 1)

                    def rotate(n):
                        i, piece = n // 3, n % 3
                        if piece < 2:
                            wait_emptied(pool, fill_of["qk", "attn", 2 * i + piece])
                            half = qk_flat[i][:, piece, :]
                            for m, table in ((0, (cos, sin)[piece]), (2, (sin, cos)[piece])):
                                nc.gpsimd.tensor_tensor(rot[i][:, m + piece, :], half, table[:, :], ALU.mult)\
                                    .then_inc(rope_step, 1)
                        else:
                            pool.wait_ge(rope_step, 4 * i + 4)
                            for m, op in ((0, ALU.subtract), (2, ALU.add)):
                                nc.gpsimd.tensor_tensor(rot[i][:, m, :], rot[i][:, m, :], rot[i][:, m + 1, :], op)\
                                    .then_inc(turned, 1)

                    for s in range(2 * UNITS + 1):
                        hidden_low(s - 1)
                        for part in norms:
                            if s == NORM[part][1] + 1:
                                inverse_deviation(part)
                            if s == NORM[part][4]:
                                add_bias(part)
                        if ahead and s in ROTATE:
                            rotate(ROTATE.index(s))

                @block.tensor
                def _(pe):
                    mm = nc.tensor.matmul

                    def scores(u):
                        half, h = (u // 4) % 2, 4 * (u // 8) + u % 4
                        if h >= 8 and h % 2 == 0:
                            pe.wait_ge(b_stacked[h // 2], 4 * 16)
                        if u >= 2:
                            pe.wait_ge(exp_done, u - 1)
                        for j in range(2):
                            c = (2 * half + j) * P
                            last = mm(ps_s[:, 2 * (u % 2) + j, :], q_stack[:, h // 2 % 4, c:c + P], k_stack[:, h % 8, :],
                                      start=True, stop=True)
                        last.then_inc(qk_done, 1)

                    def values(n, out):
                        pe.wait_ge(et_act, 4 * n + 4)
                        pe.wait_ge(et_dve, 4 * n + 4)
                        for t in range(TB):
                            for h in range(4):
                                last = mm(out[32 * h:32 * (h + 1), :], v_b[:, t, 4 * (n // 2) + h, :],
                                          et_b[:, (4 * n + h) % 5, t, :], start=(t == 0), stop=(t == TB - 1))
                        return last

                    def product(s):
                        if s not in step:
                            return
                        kind, part, i, fill = step[s]
                        if fill >= len(banks) and (kind not in ("wo", "down", "v") or i % 2 == 0):
                            wait_emptied(pe, fill - len(banks))
                        if kind in ("up", "qk", "v") and i == 0:
                            for k in range(KT):
                                wait_emptied(pe, fill_of["transpose", part, k])
                        tokens = slice(i * P, (i + 1) * P)
                        half = bank(fill)[:, (i % 2) * D:(i % 2 + 1) * D]
                        if kind == "wo":
                            for g in range(QUADS):
                                last = mm(half, heads_b[:, g, tokens], wo[:, g, :], start=(g == 0), stop=(g == QUADS - 1))
                        elif kind == "transpose":
                            pe.wait_ge(xn_ready, TB * (norms.index(part) + 1))
                            for t in range(TB):
                                last = nc.tensor.transpose(bank(fill)[:, t * P:(t + 1) * P], xn[:, t, i * P:(i + 1) * P], ident[:, :])
                        elif kind == "up":
                            todo = [(k, xs) for xs in (xh, xl) for k in range(KT)]
                            for m, (k, xs) in enumerate(todo):
                                last = mm(bank(fill), w1[:, k, i * P:(i + 1) * P], xs[:, k, :],
                                          start=(m == 0), stop=(m == len(todo) - 1))
                        elif kind == "down":
                            pe.wait_ge(h_split, FT * (ffns.index(part) + 1))
                            for f in range(FT):
                                for m, hidden in enumerate((h_hi, h_lo)):
                                    last = mm(half, hidden[:, f, tokens], w2[:, f, :],
                                              start=(f == 0 and m == 0), stop=(f == FT - 1 and m == 1))
                        elif kind == "qk":
                            last = feature_major(bank(fill), xh, xl, wb_hi, wb_lo, i * P)
                        elif kind == "v":
                            last = token_major(half, xh, xl, wb_hi, wb_lo, i, 2 * D, D)
                        elif kind == "values":
                            last = values(i, bank(fill)[:, 0:HS])
                        else:
                            pe.wait_ge(recip_ready, i + 1)
                            for j in range(2):
                                last = nc.tensor.transpose(bank(fill)[:, j * P:(j + 1) * P],
                                                           recip_b[:, j, :, :].rearrange("p h w -> p (h w)"), ident[:, :])
                        if kind not in ("wo", "down", "v") or i % 2 == 1:
                            last.then_inc(bank_filled, 1)

                    if now:
                        scores(0)
                        scores(1)
                    product(-2)
                    product(-1)
                    for u in range(UNITS):
                        if now and u + 2 < UNITS:
                            scores(u + 2)
                        product(2 * u - 0.5)
                        product(2 * u)
                        if now:
                            if u >= 1:
                                pe.wait_ge(et_act, u)
                                pe.wait_ge(et_dve, u)
                            pe.wait_ge(exp_done, u + 1)
                            unit_transposes(e_b[u % 2]).then_inc(tr_done, 1)
                        product(2 * u + 0.5)
                        product(2 * u + 1)
                    product(2 * UNITS + 0.5)
                    product(2 * UNITS + 1.5)

                @block.scalar
                def _(act):
                    def exps(u):
                        act.wait_ge(max_done, u + 1)
                        if u >= 2:
                            act.wait_ge(tr_done, u - 1)
                        exp_block(u, 0)

                    def exp_block(u, j):
                        c = (u % 4) * 2 + j
                        ins = nc.scalar.activation(e_b[u % 2][:, j, :], ps_s[:, 2 * (u % 2) + j, :], ACT.Exp,
                                                   bias=neg_max[:, u % 4, j:j + 1],
                                                   accum_out=sums[:, u // 4 % 2, c:c + 1])
                        if j == 1:
                            ins.then_inc(exp_done, 1)

                    def empty(s):
                        if s not in step:
                            return
                        kind, part, i, fill = step[s]
                        if kind == "transpose":
                            act.wait_ge(bank_filled, fill + 1)
                            nc.scalar.activation(xh[:, i, :], bank(fill), ACT.Copy).then_inc(xh_ready, 1)
                        elif kind == "up":
                            n = FT * ffns.index(part) + i
                            act.wait_ge(bank_filled, fill + 1)
                            if n >= 2:
                                act.wait_ge(h_split, n - 1)
                            emptied(nc.scalar.activation(h32[:, i % 2, :], bank(fill), ACT.Relu, bias=b1[:, i:i + 1]), fill)
                        elif kind == "qk":
                            act.wait_ge(bank_filled, fill + 1)
                            emptied(nc.scalar.activation(qk_flat[i // 2][:, i % 2, :], bank(fill), ACT.Identity,
                                                         bias=bqk[:, i:i + 1], scale=SCALE_B if i < 2 else 1.0), fill)
                        elif kind == "recip":
                            act.wait_ge(bank_filled, fill + 1)
                            if i >= 2:
                                wait_emptied(act, fill_of["values", "attn", i - 2])
                            emptied(nc.scalar.activation(rs[:, i % 2 * HS:(i % 2 + 1) * HS], bank(fill)[:, 0:HS], ACT.Copy), fill)

                    def parts_high(i, half):
                        if now and i == 0 and half == 0:
                            for pair in range(4, PAIRS):
                                act.wait_ge(b_stacked[pair], 4 * 16)
                        act.wait_ge(turned, 2 * i + half + 1)
                        high = roped_qk[:, 0, half, :, 0, :] if i == 0 else roped_qk[:, 1, half, 0, :, :]
                        nc.scalar.activation(high, rot[i][:, 2 * half:2 * half + 1, :].to_broadcast([P, 2, S]), ACT.Copy)\
                            .then_inc(high_ready, 1)

                    def others(s):
                        if ahead and s in PARTS:
                            n = PARTS.index(s)
                            parts_high(n // 2, n % 2)

                    if now:
                        exps(0)
                        exp_block(0, 1)
                    for u in range(UNITS):
                        if now and u + 1 < UNITS:
                            exps(u + 1)
                        empty(2 * u - 0.5)
                        empty(2 * u)
                        if now and u + 1 < UNITS:
                            exp_block(u + 1, 1)
                        others(2 * u)
                        if now:
                            if u >= 5:
                                act.wait_ge(bank_filled, fill_of["values", "attn", (u - 5) // 4] + 1)
                            act.wait_ge(tr_done, u + 1)
                            nc.scalar.activation(et_b[:, u % 5, 2:4, :].rearrange("p t s -> p (t s)"), ps_t[:, 1, :],
                                                 ACT.Copy).then_inc(et_act, 1)
                        empty(2 * u + 0.5)
                        empty(2 * u + 1)
                        others(2 * u + 1)
                    empty(2 * UNITS + 0.5)
                    if ahead:
                        if now:
                            act.wait_ge(bank_filled, fill_of["values", "attn", 2 * QUADS - 1] + 1)
                        for t in (1, TB - 1):
                            wait_emptied(act, fill_of["v", "attn", t])
                        nc.scalar.activation(v_b[:, :, :, 0:HB], v_next[:, :, :].rearrange("p t (h d) -> p t h d", d=HB),
                                             ACT.Copy)

                @block.vector
                def _(dve):
                    steps = [0]

                    def link(ins):
                        steps[0] += 1
                        ins.then_inc(dve_step, 1)
                        dve.wait_ge(dve_step, steps[0])

                    def statistics(part):
                        x = x_of[part]
                        if part == "ffn0":
                            dve.wait_ge(x_in, 16)
                        else:
                            kind, of = ("down", "ffn0") if part == "attn" else ("wo", "ffn1")
                            for t in (1, TB - 1):
                                wait_emptied(dve, fill_of[kind, of, t])
                        for t in range(TB):
                            ins = nc.vector.bn_stats(stats[:, t, :], x[:, t, :])
                        ins.then_inc(stats_ready, 1)

                    def aggregate(part):
                        dve.wait_ge(stats_ready, norms.index(part) + 1)
                        for t in range(TB):
                            ins = nc.vector.bn_aggr(mean_var[:, t, :], stats[:, t, :])
                        link(ins)
                        nc.vector.tensor_scalar(rstd[:, :], mean_var[:, :, 1], EPS, None, ALU.add).then_inc(var_ready, 1)

                    def normalise(part):
                        dve.wait_ge(rstd_ready, norms.index(part) + 1)
                        normalise_blocks(part, 0)

                    def normalise_rest(part):
                        normalise_blocks(part, TB // 2)
                        dve.wait_ge(xn_ready, TB * (norms.index(part) + 1))

                    def normalise_blocks(part, first):
                        for t in range(first, first + TB // 2):
                            nc.vector.tensor_scalar(xn[:, t, :], x_of[part][:, t, :], mean_var[:, t, 0:1], rstd[:, t:t + 1],
                                                    ALU.subtract, ALU.mult).then_inc(xn_ready, 1)

                    def parts_low(i, half):
                        dve.wait_ge(high_ready, 2 * i + half + 1)
                        if i == 0:
                            high, low = roped_qk[:, 0, half, :, 0, :], roped_qk[:, 0, half, :, 1, :]
                        else:
                            high, low = roped_qk[:, 1, half, 0, :, :], roped_qk[:, 1, half, 1, :, :]
                        nc.vector.tensor_tensor(low, rot[i][:, 2 * half:2 * half + 1, :].to_broadcast([P, 2, S]), high,
                                                ALU.subtract).then_inc(roped, 1)

                    def unit_max(u):
                        dve.wait_ge(qk_done, u + 1)
                        nc.vector.reduce_max(neg_max[:, u % 4, :], ps_s[:, 2 * (u % 2):2 * (u % 2) + 2, :], AX.X, negate=True)\
                            .then_inc(max_done, 1)

                    def invert(n):
                        dve.wait_ge(exp_done, 4 * n + 4)
                        if n >= 1:
                            dve.wait_ge(bank_filled, fill_of["recip", "attn", n - 1] + 1)
                        link(nc.vector.reciprocal(recip[:, n % 2, 0:8], sums[:, n % 2, 0:8]))
                        src = recip[:, n % 2, 0:8].rearrange("p (h j o) -> p j h o", j=2, o=1)
                        nc.vector.tensor_copy(recip_b[:, :, :, :], src.to_broadcast([P, 2, 4, 32])).then_inc(recip_ready, 1)

                    def empty(s):
                        if s not in step:
                            return
                        kind, part, i, fill = step[s]
                        both = bank(fill).rearrange("p (t d) -> p t d", d=D)
                        if kind == "transpose":
                            n = KT * norms.index(part) + i
                            dve.wait_ge(xh_ready, n + 1)
                            emptied(nc.vector.tensor_tensor(xl[:, i, :], bank(fill), xh[:, i, :], ALU.subtract), fill)
                        elif kind in ("wo", "down") and i % 2 == 1:
                            if kind == "wo":
                                dve.wait_ge(before_in, 16)
                            else:
                                dve.wait_ge(biased, norms.index(part) + 1)
                            dve.wait_ge(bank_filled, fill + 1)
                            x = x_of[part][:, i - 1:i + 1, :]
                            emptied(nc.vector.tensor_tensor(x, x, both, ALU.add), fill)
                        elif kind == "v" and i % 2 == 1:
                            dve.wait_ge(bank_filled, fill + 1)
                            bias = bv_rows[:, :].rearrange("p (o d) -> p o d", o=1).to_broadcast([P, 2, D])
                            emptied(nc.vector.tensor_tensor(v_next[:, i - 1:i + 1, :], both, bias, ALU.add), fill)
                        elif kind == "values":
                            dve.wait_ge(bank_filled, fill + 1)
                            wait_emptied(dve, fill_of["recip", "attn", i])
                            queries = slice(i % 2 * HS, (i % 2 + 1) * HS)
                            emptied(nc.vector.tensor_tensor(heads_b[:, i // 2, queries], bank(fill)[:, 0:HS], rs[:, queries],
                                                            ALU.mult), fill)

                    def hidden_high(s):
                        if s in step and step[s][0] == "up":
                            kind, part, i, fill = step[s]
                            wait_emptied(dve, fill)
                            if part == "ffn1" and ahead and i == 0:
                                dve.wait_ge(rope_step, 8)
                            if part == "ffn1" and ahead and i == FT // 2:
                                dve.wait_ge(roped, 4)
                            nc.vector.tensor_copy(h_hi[:, i, :], h32[:, i % 2, :]).then_inc(hi_copied, 1)

                    def others(s):
                        for part in norms:
                            for n, work in enumerate((statistics, aggregate, normalise, normalise_rest)):
                                if s == NORM[part][n]:
                                    work(part)
                        if ahead and s in LOWS:
                            n = LOWS.index(s)
                            parts_low(n // 2, n % 2)

                    if now:
                        unit_max(0)
                        unit_max(1)
                    empty(-1)
                    for u in range(UNITS):
                        if now and u % 4 == 0 and u:
                            invert(u // 4 - 1)
                        if now and u + 2 < UNITS:
                            unit_max(u + 2)
                        empty(2 * u - 0.5)
                        empty(2 * u)
                        hidden_high(2 * u - 1)
                        others(2 * u)
                        if now:
                            if u >= 5:
                                dve.wait_ge(bank_filled, fill_of["values", "attn", (u - 5) // 4] + 1)
                            dve.wait_ge(tr_done, u + 1)
                            nc.vector.tensor_copy(et_b[:, u % 5, 0:2, :].rearrange("p t s -> p (t s)"), ps_t[:, 0, :])\
                                .then_inc(et_dve, 1)
                        empty(2 * u + 0.5)
                        empty(2 * u + 1)
                        hidden_high(2 * u)
                        others(2 * u + 1)
                    if now:
                        invert(2 * QUADS - 1)
                    empty(2 * UNITS + 1.5)

            next_block()

        XT0 = 5
        UP0 = (8, 9, 10, 11, 12, 13, 15, 16)
        DOWN0 = (18, 20, 21, 22)
        XTB = 26
        QK = (29, 30, 31, 33)
        VB = (35, 36, 37, 39)
        XT1 = 40
        UP1 = (43, 44, 45, 46, 47, 49, 51, 52)
        DOWN1 = (55, 56, 58, 59)
        ROTATE = (30, 31, 34, 36, 37, 39)
        PARTS = (35, 37, 41, 42)
        LOWS = (36, 40, 42, 46)
        NORM = {"ffn0": (0, 0, 3, 3, 5), "attn": (22, 23, 24, 24, 28), "ffn1": (29, 29, 33, 33, 39)}

        attention_b(-1, False, False, True)
        attention_b(0, False, True, True)
        with nc.Fori(1, BATCH - 1) as seq:
            attention_b(seq, True, True, True)
        attention_b(BATCH - 1, True, True, False)
        attention_b(BATCH, True, False, False)


def kernel(**inputs):
    import numpy as np
    import concourse.bacc as bacc
    from concourse.bass_utils import run_bass_kernel_spmd

    def get(name):
        return np.asarray(inputs["L0_" + name])

    half, tokens = 8, 512
    pos = np.arange(tokens, dtype=np.float32)[:, None]
    freq = np.float32(1.0) / np.float32(10000.0) ** (np.arange(half, dtype=np.float32) / np.float32(half))
    angles = (pos * freq[None, :]).astype(np.float32)
    cos = np.ascontiguousarray(np.tile(np.cos(angles).astype(np.float32).T, (16, 1)))
    sin = np.ascontiguousarray(np.tile(np.sin(angles).astype(np.float32).T, (16, 1)))

    def halves(w):
        lead = w.shape[:-1]
        return np.swapaxes(w.reshape(*lead, 16, 2, 8), -3, -2).reshape(*lead, 256)

    wb = np.concatenate([halves(get("attn_b_wq_w")), halves(get("attn_b_wk_w")), get("attn_b_wv_w")], axis=1)
    bqk = np.concatenate([halves(get("attn_b_wq_b")), halves(get("attn_b_wk_b"))]).reshape(4, 128).T
    wo = get("attn_b_wo_w").reshape(4, 4, 16, 256).transpose(1, 2, 0, 3)
    arrays = {
        "X": get("attn_a_X"), "WQ": get("attn_a_Wq"), "WK": get("attn_a_Wk"), "WV": get("attn_a_Wv"),
        "WPOST": get("attn_a_Wpost"), "WB": wb, "BQK": bqk, "BV": get("attn_b_wv_b").reshape(1, 256), "WO": wo,
        "BO": get("attn_b_wo_b").reshape(1, 256), "W1T": get("ffn_W1").T, "B1": get("ffn_b1").reshape(8, 128).T,
        "W2T": get("ffn_W2").T, "B2": get("ffn_b2").reshape(1, 256), "COS": cos, "SIN": sin,
    }
    arrays = {name: np.ascontiguousarray(a) for name, a in arrays.items()}
    nc = bacc.Bacc("TRN2", target_bir_lowering=False, num_devices=1)
    args = [nc.dram_tensor(name, a.shape, mybir.dt.from_np(a.dtype), kind="ExternalInput").ap()
            for name, a in arrays.items()]
    x1 = nc.dram_tensor("X1", arrays["X"].shape, mybir.dt.float32, kind="Internal").ap()
    out = nc.dram_tensor("OUT", arrays["X"].shape, mybir.dt.float32, kind="ExternalOutput").ap()
    hybrid_block_kernel(nc, *args, x1, out)
    r = run_bass_kernel_spmd(nc, [arrays], core_ids=[0])
    return r.results[0]["OUT"]
```
